# Optimizing a Trainium2 kernel written in Bass

```python
import numpy as np
import jax
import jax.numpy as jnp

def _softmax(x, axis=-1):
    return jax.nn.softmax(x, axis=axis)

def _gelu(x):
    return jax.nn.gelu(x, approximate=True)

def _silu(x):
    return jax.nn.silu(x)

def _sigmoid(x):
    return jax.nn.sigmoid(x)

def _layernorm(x, axis=-1, eps=1e-05):
    m = jnp.mean(x, axis=axis, keepdims=True)
    v = jnp.var(x, axis=axis, keepdims=True)
    return (x - m) / jnp.sqrt(v + eps)

def _scatter_add(tgt, idx, src, axis=0):
    return tgt.at[idx].add(src)

def _segment_sum(src, seg, n):
    return jax.ops.segment_sum(src, seg, n)
kernel_name = 'mk_gnn_resnorm_d1_gnn_r8_35aaa1'

def setup_inputs(seed: int=0):
    np.random.seed(seed)
    _w = jnp.asarray

    def _rec_inputs():
        import jax
        import jax.numpy as jnp
        _gk = jax.random.key(seed)
        x = -0.0005121 + 1.001 * jax.random.normal(jax.random.fold_in(_gk, 1), (6250, 64), jnp.float32)
        src = jax.random.randint(jax.random.fold_in(_gk, 2), (200000,), 0, 6250, jnp.int32)
        dst = jax.random.randint(jax.random.fold_in(_gk, 3), (200000,), 0, 6250, jnp.int32)
        _o = jnp.argsort(dst, stable=True)
        src = src[_o]
        dst = dst[_o]
        edge_attr_64 = -9.77346e-05 + 0.999888 * jax.random.normal(jax.random.fold_in(_gk, 12), (200000, 64), jnp.float32)
        return (x, src, dst, edge_attr_64)
    x, src, dst, edge_attr_64 = _rec_inputs()

    def _L0_gnn_setup():
        import jax, jax.numpy as jnp
        import numpy as np
        N_NODES = 6250
        N_EDGES = 100000
        D_EDGE = 64
        D_NODE = 64
        D_IN = 2 * D_EDGE + D_NODE
        D_HID = 256
        D_OUT = 64
        key = jax.random.key(seed)
        ks = jax.random.split(key, 6)
        node_feat = jax.random.normal(ks[0], (N_NODES, D_NODE), dtype=jnp.float32)
        edge_feat = jax.random.normal(ks[1], (N_EDGES, D_EDGE), dtype=jnp.float32)
        senders = jax.random.randint(ks[2], (N_EDGES,), 0, N_NODES, dtype=jnp.int32)
        receivers = jax.random.randint(ks[3], (N_EDGES,), 0, N_NODES, dtype=jnp.int32)
        W1 = jax.random.normal(ks[4], (D_IN, D_HID), dtype=jnp.float32) * (1.0 / np.sqrt(D_IN))
        b1 = jnp.zeros((D_HID,), dtype=jnp.float32)
        W2 = jax.random.normal(ks[5], (D_HID, D_OUT), dtype=jnp.float32) * (1.0 / np.sqrt(D_HID))
        b2 = jnp.zeros((D_OUT,), dtype=jnp.float32)
        return {'node_feat': node_feat, 'edge_feat': edge_feat, 'senders': senders, 'receivers': receivers, 'W1': W1, 'b1': b1, 'W2': W2, 'b2': b2}
    _L0_gnn_all = _L0_gnn_setup()
    _L0_gnn_in = {k: v for k, v in _L0_gnn_all.items() if k in ('W1', 'b1', 'W2', 'b2')}
    del _L0_gnn_all
    return {'x': x, 'src': src, 'dst': dst, 'edge_attr_64': edge_attr_64, 'L0_gnn_W1': _L0_gnn_in['W1'], 'L0_gnn_b1': _L0_gnn_in['b1'], 'L0_gnn_W2': _L0_gnn_in['W2'], 'L0_gnn_b2': _L0_gnn_in['b2']}

def reference(x, src, dst, edge_attr_64, L0_gnn_W1, L0_gnn_b1, L0_gnn_W2, L0_gnn_b2):
    import jax
    import jax.numpy as jnp

    def _L0_gnn_ref(node_feat, edge_feat, senders, receivers, W1, b1, W2, b2):
        import jax, jax.numpy as jnp
        import numpy as np
        N_NODES = 6250
        N_EDGES = 100000
        D_EDGE = 64
        D_NODE = 64
        D_IN = 2 * D_EDGE + D_NODE
        D_HID = 256
        D_OUT = 64
        in_agg = jax.ops.segment_sum(edge_feat, receivers, num_segments=N_NODES)
        out_agg = jax.ops.segment_sum(edge_feat, senders, num_segments=N_NODES)
        to_updater = jnp.concatenate([in_agg, out_agg, node_feat], axis=1)
        h = jax.nn.relu(to_updater @ W1 + b1)
        return h @ W2 + b2
    x = _layernorm(x + _L0_gnn_ref(x, edge_attr_64, src, dst, L0_gnn_W1, L0_gnn_b1, L0_gnn_W2, L0_gnn_b2), axis=-1)
    return x

_drawn_inputs = setup_inputs


def setup_inputs(seed=0):
    import zlib

    import numpy as np

    out = dict(_drawn_inputs(seed))
    spreads = {'L0_gnn_b1': (0.0, 0.355), 'L0_gnn_b2': (0.0, 0.281)}
    factors = {}
    for name, (base, spread) in spreads.items():
        noise = np.random.default_rng([zlib.crc32(name.encode()), seed]).standard_normal(out[name].shape)
        drawn = base * np.exp(spread * noise) if base else spread * noise
        out[name] = jnp.asarray(drawn.astype(out[name].dtype))
    for name, factor in factors.items():
        out[name] = (out[name] * factor).astype(out[name].dtype)
    return out
```

```python
from contextlib import ExitStack

import concourse.bass as bass
from concourse import mybir
from concourse.alu_op_type import AluOpType as ALU

N_NODES = 6250
N_EDGES = 200000
D = 64
D_HID = 256
P = 128
EPS = 1e-05

COLS = 16
QUAD = 4
QUADS = COLS // QUAD
CHUNK = P * COLS
N_CHUNKS = -(-N_EDGES // CHUNK)
LAST_EDGES = N_EDGES - (N_CHUNKS - 1) * CHUNK
LAST_PARTS = LAST_EDGES // COLS
PAD = CHUNK - LAST_EDGES
PAIRS = N_CHUNKS // 2
assert N_CHUNKS % 2 == 0 and LAST_EDGES % COLS == 0 and PAD <= LAST_EDGES

OUT_TABLES = 8
TABLE_ROWS = 6400
SPARE = N_NODES
assert TABLE_ROWS >= N_NODES + P and TABLE_ROWS % P == 0

NT = N_NODES // P
N_TILES = NT + 1
REST = N_NODES - NT * P
POW = 60


def build(nc, x, src, dst, edges, w1, b1, w2, b2, consts, out):
    fp32 = mybir.dt.float32
    bf16 = mybir.dt.bfloat16
    i32 = mybir.dt.int32
    ACT = mybir.ActivationFunctionType
    AX = mybir.AxisListType

    out_tab = [nc.dram_tensor(f"out_table{k}", (TABLE_ROWS, D), fp32, kind="Internal").ap()
               for k in range(OUT_TABLES)]
    in_tab = nc.dram_tensor("in_table", (TABLE_ROWS, D), fp32, kind="Internal").ap()

    with ExitStack() as ctx:
        def sb(name, shape, dt=fp32):
            return ctx.enter_context(nc.sbuf_tensor(name, shape, dt))

        def ps(name, shape):
            return ctx.enter_context(nc.psum_tensor(name, shape, fp32))

        def sem(name):
            return ctx.enter_context(nc.semaphore(name))

        cst = sb("cst", [P, 2 * P + 3])
        ident = cst[:, 0:P]
        iota = cst[:, P:2 * P]
        weight = cst[:, 2 * P:2 * P + 1]
        unweight = cst[:, 2 * P + 1:2 * P + 2]
        part_no = cst[:, 2 * P + 2:2 * P + 3]
        spare_row = sb("spare_row", [P, 1])
        ident_bf = sb("ident_bf", [P, P], bf16)
        ones = sb("ones", [P, P])
        zeros = sb("zeros", [P, TABLE_ROWS // P * D])

        rows_i = [sb(f"rows_i{n}", [N_CHUNKS, CHUNK], i32) for n in range(2)]
        part_i = sb("part_i", [N_CHUNKS, CHUNK], i32)
        rows_f = sb("rows_f", [N_CHUNKS, CHUNK])
        rows_hi = [sb(f"rows_hi{n}", [N_CHUNKS, CHUNK], bf16) for n in range(2)]
        rows_lo = [sb(f"rows_lo{n}", [N_CHUNKS, CHUNK], bf16) for n in range(2)]
        cols_f = [sb(f"cols_f{n}", [P, N_CHUNKS, COLS]) for n in range(2)]
        lowest = sb("lowest", [N_CHUNKS, 1])
        highest = sb("highest", [N_CHUNKS, 1])
        wide = sb("wide", [N_CHUNKS, 1])
        diag = sb("diag", [N_CHUNKS, N_CHUNKS])
        base = sb("base", [P, N_CHUNKS])
        off_base = sb("off_base", [P, N_CHUNKS])
        win_rows = sb("win_rows", [P, N_CHUNKS], i32)
        shift = sb("shift", [P, 1])
        flag_i = sb("flag_i", [P, 1], i32)

        feat = [sb(f"feat{b}", [P, COLS, D]) for b in range(2)]
        same = [sb(f"same{b}", [P, QUAD, P]) for b in range(2)]
        onehot = [sb(f"onehot{b}", [P, QUAD, P]) for b in range(2)]
        rel = [sb(f"rel{b}", [P, COLS]) for b in range(2)]
        payload = [sb(f"payload{b}", [P, COLS, D + 1]) for b in range(2)]
        win_pay = [sb(f"win_pay{b}", [P, D]) for b in range(2)]
        repeated = sb("repeated", [P, COLS])
        target = [sb(f"target{b}", [P, COLS], i32) for b in range(2)]

        w1io = sb("w1io", [P, D_HID])
        w1x = sb("w1x", [D, D_HID])
        w2s = sb("w2s", [P, 2, D])
        b1s = sb("b1s", [P, 2])
        b2s = sb("b2s", [P, D])
        xs = sb("xs", [P, N_TILES, D])

        bank = [ps(f"bank{n}", [P, 512]) for n in range(8)]
        ps_nodes = bank[0:2]
        ps_pay = bank[2:4]
        ps_win = bank[4:6]

        s_cst = sem("s_cst")
        s_row = [sem(f"s_row{n}") for n in range(2)]
        s_w = sem("s_w")
        s_x = sem("s_x")
        s_xz = sem("s_xz")
        s_one = sem("s_one")
        s_zero = sem("s_zero")
        s_pad = sem("s_pad")
        s_pre = sem("s_pre")
        s_tp = sem("s_tp")
        s_te = sem("s_te")
        s_b = sem("s_b")
        s_rows = sem("s_rows")
        s_feat = [sem(f"s_feat{b}") for b in range(2)]
        s_nodes = sem("s_nodes")
        s_same = sem("s_same")
        s_hot = sem("s_hot")
        s_rel = sem("s_rel")
        s_pay = sem("s_pay")
        s_quad = sem("s_quad")
        s_ev = sem("s_ev")
        s_wev = sem("s_wev")
        s_rep = sem("s_rep")
        s_tgt = sem("s_tgt")
        s_free = sem("s_free")
        s_tab = [sem(f"s_tab{k}") for k in range(OUT_TABLES)]
        s_in = sem("s_in")
        s_agg = sem("s_agg")

        GROUPS = [(a, min(a + 4, N_TILES)) for a in range(0, N_TILES, 4)]
        NSEG = 4
        SEG = NT // NSEG
        seg_cols = SEG * D
        tabs = [sb(f"tabs{b}", [P, OUT_TABLES, seg_cols]) for b in range(2)]
        agg_in = sb("agg_in", [P, N_TILES, D])
        agg_out = zeros[:, 0:N_TILES * D].rearrange("p (r d) -> p r d", d=D)
        catT = sb("catT", [P, 512])
        xT = sb("xT", [D, 512])
        hid = sb("hid", [P, 2, 512])
        y = sb("y", [P, N_TILES, D])
        stats = sb("stats", [P, 4, 6])
        mv = sb("mv", [P, 4, 2])
        sd = sb("sd", [P, 4])
        rstd = sb("rstd", [P, 4])

        win_now = [sb(f"win_now{b}", [P, 1], i32) for b in range(2)]
        eps = sb("eps", [P, 1])
        PRE_FLAG = 13
        s_seg = [sem(f"s_seg{n}") for n in range(2)]
        s_sum = sem("s_sum")
        s_nt = sem("s_nt")
        s_nte = sem("s_nte")
        s_h = sem("s_h")
        s_hr = sem("s_hr")
        s_o = sem("s_o")
        s_xb = sem("s_xb")
        s_y = sem("s_y")
        s_st = sem("s_st")
        s_ag = sem("s_ag")
        s_sd = sem("s_sd")
        s_rs = sem("s_rs")
        s_ln = sem("s_ln")
        s_out = sem("s_out")

        block = ctx.enter_context(nc.Block())

        def seed(e):
            pass

        row_view = [v[0:(N_CHUNKS - 1) * CHUNK].rearrange("(c k) -> c k", k=CHUNK) for v in (src, dst)]
        TB = 5
        TBATCH = [(n, a, min(a + TB, COLS)) for n in range(2) for a in range(0, COLS, TB)]

        def nodes_view(t, s):
            if s < NSEG:
                return t[0:NT * P, :].rearrange("(p r) d -> p (r d)", r=NT)[:, s * seg_cols:(s + 1) * seg_cols]
            return t[NT * P:(NT + 1) * P, :] if t.shape[0] >= (NT + 1) * P else t[NT * P:, :]

        def load_segment(e, s):
            b, n = s % 2, seg_cols if s < NSEG else D
            for k in range(OUT_TABLES):
                e.dma_start(tabs[b][:, k, 0:n], nodes_view(out_tab[k], s)).then_inc(s_seg[b], 16)
            to = agg_in[:, s * SEG:(s + 1) * SEG, :] if s < NSEG else agg_in[:, NT:NT + 1, :]
            e.dma_start(to.rearrange("p r d -> p (r d)"), nodes_view(in_tab, s)).then_inc(s_seg[b], 16)

        @block.sync
        def _(e):
            e.dma_start(cst[:, :], consts).then_inc(s_cst, 16)
            for n, v in enumerate((src, dst)):
                full = (N_CHUNKS - 1) // 16 * 16
                e.dma_start(rows_i[n][0:full, :], row_view[n][0:full, :]).then_inc(s_row[n], 16)
                e.dma_start(rows_i[n][full:N_CHUNKS - 1, :], row_view[n][full:, :]).then_inc(s_row[n], 16)
                last = v[(N_CHUNKS - 1) * CHUNK:N_EDGES].rearrange("(a k) -> a k", a=1)
                e.dma_start(rows_i[n][N_CHUNKS - 1:N_CHUNKS, 0:LAST_EDGES], last).then_inc(s_row[n], 16)
                e.dma_start(rows_i[n][N_CHUNKS - 1:N_CHUNKS, LAST_EDGES:CHUNK],
                            last[:, LAST_EDGES - PAD:LAST_EDGES]).then_inc(s_row[n], 16)

            def load_chunks(pair, first_chunk, last_pair):
                for b in range(2):
                    c = first_chunk + b
                    e.wait_ge(s_quad, QUADS * c + 1)
                    if last_pair and b == 1:
                        e.wait_ge(s_pad, 1 if first_chunk == N_CHUNKS - 2 else 2)
                        e.dma_start(feat[b][0:LAST_PARTS, :, :],
                                    edges[(N_CHUNKS - 1) * CHUNK:N_EDGES, :].rearrange(
                                        "(p j) d -> p j d", j=COLS)).then_inc(s_feat[b], 16)
                    else:
                        at = (2 * pair + b) * CHUNK
                        e.dma_start(feat[b][:, :, :],
                                    edges[bass.ds(at, CHUNK), :].rearrange(
                                        "(p j) d -> p j d", j=COLS)).then_inc(s_feat[b], 16)

            def all_chunks(offset):
                with e.Fori(offset, offset + PAIRS - 1) as i:
                    load_chunks(i - offset, 2 * i, False)
                load_chunks(PAIRS - 1, 2 * (offset + PAIRS - 1), True)

            all_chunks(0)
            e.wait_ge(s_pre, PRE_FLAG)
            again = e.value_load(flag_i[0:1, 0:1], min_val=0, max_val=1)
            with e.If(again > 0):
                all_chunks(PAIRS)

            e.wait_ge(s_agg, 1)
            for s in range(NSEG + 1):
                if s >= 2:
                    e.wait_ge(s_sum, 2 * (s - 1))
                load_segment(e, s)
            e.wait_ge(s_out, 16 * (NSEG + 1))

        @block.gpsimd
        def _(e):
            e.sem_inc(s_free, 3)
            e.wait_ge(s_zero, 1)
            for k in range(OUT_TABLES):
                e.dma_start(out_tab[k].rearrange("(p r) d -> p (r d)", p=P), zeros[:, :]).then_inc(s_tab[k], 16)
            e.dma_start(in_tab.rearrange("(p r) d -> p (r d)", p=P), zeros[:, :]).then_inc(s_in, 16)

            def add_chunk(c, b, d, window):
                e.wait_ge(s_tgt, c + 1)
                for t in range(COLS):
                    if t % QUAD == 0:
                        e.wait_ge(s_ev, QUADS * c + t // QUAD + 3)
                    at = bass.IndirectOffsetOnAxis(ap=target[b][:, t:t + 1], axis=0)
                    if window:
                        k, turn = t % OUT_TABLES, COLS // OUT_TABLES * c + t // OUT_TABLES
                        e.wait_ge(s_tab[k], 16 * turn + 16)
                        e.nop(nofuse=True)
                        e.indirect_dma_start(out_tab[k], at, payload[b][:, t, 0:D], None,
                                             compute_op=ALU.add).then_inc(s_tab[k], 16)
                    else:
                        e.wait_ge(s_in, 16 * (COLS * (c - N_CHUNKS) + t + N_CHUNKS + 1))
                        e.nop(nofuse=True)
                        e.indirect_dma_start(in_tab, at, payload[b][:, t, 0:D], None,
                                             compute_op=ALU.add).then_inc(s_in, 16)
                    if t == COLS // 2 - 2:
                        if window:
                            e.wait_ge(s_wev, c + 3)
                            e.wait_ge(s_in, 16 * c + 16)
                            e.nop(nofuse=True)
                            e.indirect_dma_start(
                                in_tab, bass.IndirectOffsetOnAxis(ap=win_now[b][:, 0:1], axis=0),
                                win_pay[b][:, :], None, compute_op=ALU.add).then_inc(s_in, 16)
                    if t % (COLS // 2) == COLS // 2 - 1:
                        e.sem_inc(s_free, 1)

            with e.Fori(0, PAIRS) as i:
                for b in range(2):
                    add_chunk(2 * i + b, b, 2 * i + b, True)
            e.wait_ge(s_pre, PRE_FLAG)
            again = e.value_load(flag_i[0:1, 0:1], min_val=0, max_val=1)
            with e.If(again > 0):
                with e.Fori(PAIRS, 2 * PAIRS) as i:
                    for b in range(2):
                        add_chunk(2 * i + b, b, 2 * i + b - N_CHUNKS, False)
                e.wait_ge(s_in, 16 * (COLS * N_CHUNKS + N_CHUNKS + 1))
            for k in range(OUT_TABLES):
                e.wait_ge(s_tab[k], 16 * (COLS * N_CHUNKS // OUT_TABLES + 1))
            e.wait_ge(s_in, 16 * (N_CHUNKS + 1))
            e.sem_inc(s_agg, 1)

        @block.scalar
        def _(e):
            e.dma_start(w1io[:, :], w1[0:2 * D, :]).then_inc(s_w, 16)
            e.dma_start(w1x[:, :], w1[2 * D:3 * D, :]).then_inc(s_w, 16)
            e.dma_start(w2s[:, :, :], w2.rearrange("(a p) n -> p a n", p=P)).then_inc(s_w, 16)
            with nc.allow_non_contiguous_dma(reason="256 biases, once"):
                e.dma_start(b1s[:, :], b1.rearrange("(a p) -> p a", p=P)).then_inc(s_w, 16)
            e.dma_start(b2s[:, :], b2.rearrange("(a n) -> a n", a=1).to_broadcast([P, D])).then_inc(s_w, 16)
            e.wait_ge(s_xz, 1)
            e.dma_start(xs[:, 0:NT, :].rearrange("p r d -> p (r d)"),
                        x[0:NT * P, :].rearrange("(p r) d -> p (r d)", r=NT)).then_inc(s_x, 16)
            e.dma_start(xs[0:REST, NT, :], x[NT * P:, :]).then_inc(s_x, 16)

            e.sem_inc(s_ev, 2)
            e.sem_inc(s_wev, 2)

            def evacuate_chunk(c, b, window):
                for q in range(QUADS):
                    if q % 2 == 0:
                        e.wait_ge(s_free, 2 * c + q // 2 + 1)
                    e.wait_ge(s_pay, QUADS * c + q + 1)
                    e.activation(payload[b][:, QUAD * q:QUAD * (q + 1), :],
                                 ps_pay[q % 2][:, 0:QUAD * (D + 1)].rearrange("p (t d) -> p t d", d=D + 1),
                                 ACT.Copy).then_inc(s_ev, 1)
                if window:
                    e.wait_ge(s_quad, QUADS * c + 9)
                    e.activation(win_pay[b][:, :], ps_win[b][:, 0:D], ACT.Copy).then_inc(s_wev, 1)

            with e.Fori(0, PAIRS) as i:
                for b in range(2):
                    evacuate_chunk(2 * i + b, b, True)
            e.wait_ge(s_pre, PRE_FLAG)
            again = e.value_load(flag_i[0:1, 0:1], min_val=0, max_val=1)
            with e.If(again > 0):
                with e.Fori(PAIRS, 2 * PAIRS) as i:
                    for b in range(2):
                        evacuate_chunk(2 * i + b, b, False)

            e.wait_ge(s_w, 16 * 5)
            for g, (a, z) in enumerate(GROUPS):
                n = P * (z - a)
                e.wait_ge(s_nt, g + 1)
                if g:
                    e.wait_ge(s_h, 2 * g)
                e.activation(catT[:, 0:n], bank[0][:, 0:n], ACT.Copy)
                e.activation(xT[:, 0:n], bank[1][0:D, 0:n], ACT.Copy).then_inc(s_nte, 1)
                for m in range(2):
                    e.wait_ge(s_h, 2 * g + m + 1)
                    if g:
                        e.wait_ge(s_o, g)
                    e.activation(hid[:, m, 0:n], bank[2 + m][:, 0:n], ACT.Relu,
                                 bias=b1s[:, m:m + 1]).then_inc(s_hr, 1)
                e.wait_ge(s_ag, g + 1)
                if g:
                    e.wait_ge(s_rs, g)
                e.activation(sd[:, 0:z - a], mv[:, 0:z - a, 1], ACT.Sqrt, bias=eps[:, 0:1]).then_inc(s_sd, 1)
                if z == N_TILES or (a // SEG != z // SEG):
                    pass
            for s in range(NSEG + 1):
                e.wait_ge(s_ln, -(-min((s + 1) * SEG, N_TILES) // 4) if s < NSEG else len(GROUPS))
                if s < NSEG:
                    to = out[0:NT * P, :].rearrange("(p r) d -> p (r d)", r=NT)
                    e.dma_start(to[:, s * seg_cols:(s + 1) * seg_cols],
                                y[:, s * SEG:(s + 1) * SEG, :].rearrange("p r d -> p (r d)")).then_inc(s_out, 16)
                else:
                    e.dma_start(out[NT * P:, :], y[0:REST, NT, :]).then_inc(s_out, 16)

        def node_group(e, g, a, z):
            n = z - a
            e.wait_ge(s_o, g + 1)
            e.tensor_tensor(y[:, a:z, :], y[:, a:z, :], bank[4][:, 0:n * D].rearrange("p (t d) -> p t d", d=D),
                            ALU.add).then_inc(s_y, 1)
            e.wait_ge(s_y, g + 1)
            for t in range(n):
                last = e.bn_stats(stats[:, t, :], y[:, a + t, :])
            last.then_inc(s_st, 1)
            e.wait_ge(s_st, g + 1)
            if g:
                e.wait_ge(s_sd, g)
            for t in range(n):
                last = e.bn_aggr(mv[:, t, :], stats[:, t, :])
            last.then_inc(s_ag, 1)
            e.wait_ge(s_sd, g + 1)
            e.reciprocal(rstd[:, 0:n], sd[:, 0:n]).then_inc(s_rs, 1)
            e.wait_ge(s_rs, g + 1)
            for t in range(n):
                last = e.tensor_scalar(y[:, a + t, :], y[:, a + t, :], mv[:, t, 0:1], rstd[:, t:t + 1],
                                       ALU.subtract, ALU.mult)
            last.then_inc(s_ln, 1)

        @block.vector
        def _(e):
            steps = [0]

            def step(ins):
                steps[0] += 1
                ins.then_inc(s_pre, 1)
                e.wait_ge(s_pre, steps[0])

            e.memset(zeros[:, :], 0.0).then_inc(s_zero, 1)
            e.memset(ones[:, :], 1.0).then_inc(s_one, 1)
            e.memset(eps[:, :], EPS).then_inc(s_one, 1)
            e.memset(xs[96:P, NT, :], 0.0).then_inc(s_xz, 1)
            e.sem_inc(s_quad, QUADS + 1)
            e.wait_ge(s_cst, 16)
            e.tensor_copy(ident_bf[:, :], ident).then_inc(s_one, 1)
            step(e.tensor_scalar(spare_row[:, :], part_no, float(SPARE), None, ALU.add))
            for n in range(2):
                e.wait_ge(s_row[n], 64)
                if n == 1:
                    e.wait_ge(s_tp, 4)
                step(e.tensor_copy(rows_f[:, :], rows_i[n][:, :]))
                step(e.tensor_scalar(part_i[:, :], rows_i[n][:, :], 0x1F80, None, ALU.bitwise_and))
                e.tensor_copy(rows_hi[n][:, :], part_i[:, :])
                e.tensor_tensor(rows_lo[n][:, :], rows_i[n][:, :], part_i[:, :], ALU.subtract).then_inc(s_rows, 1)
                for w, (nn, a, z) in enumerate(TBATCH):
                    if nn == n:
                        e.wait_ge(s_tp, w + 1)
                        e.tensor_copy(cols_f[n][:, :, a:z].rearrange("p c j -> p j c"),
                                      bank[w % 4][:, 0:(z - a) * N_CHUNKS].rearrange(
                                          "p (j c) -> p j c", c=N_CHUNKS)).then_inc(s_te, 1)
                e.wait_ge(s_te, 4 * (n + 1))
                e.wait_ge(s_rows, n + 1)
            step(e.tensor_reduce(lowest[:, :], rows_f[:, :], AX.X, ALU.min))
            step(e.tensor_reduce(highest[:, :], rows_f[:, :], AX.X, ALU.max))
            step(e.tensor_tensor(wide[:, :], highest[:, :], lowest[:, :], ALU.subtract))
            step(e.tensor_scalar(wide[:, :], wide[:, :], P - 0.5, None, ALU.is_gt))
            step(e.tensor_scalar(diag[:, :], ident[0:N_CHUNKS, 0:N_CHUNKS], lowest[:, 0:1], None, ALU.mult))
            e.wait_ge(s_b, 1)
            step(e.tensor_copy(base[:, :], bank[4][:, 0:N_CHUNKS]))
            step(e.tensor_scalar(shift[:, :], bank[5][:, 0:1], 0.5, None, ALU.is_gt))
            step(e.tensor_copy(flag_i[:, :], shift[:, :]))
            assert steps[0] == PRE_FLAG
            step(e.tensor_scalar(shift[:, :], shift[:, :], float(1 << 14), None, ALU.mult))
            step(e.tensor_scalar(off_base[:, :], base[:, :], shift[:, 0:1], None, ALU.subtract))
            step(e.tensor_scalar(win_rows[:, :], base[:, :], part_no, None, ALU.add))

            def chunk(c, b, d, n, window):
                if window:
                    e.wait_ge(s_quad, QUADS * c + 1)
                    e.tensor_scalar(rel[b][:, :], cols_f[1][:, bass.ds(d, 1), :].rearrange("p a j -> p (a j)"),
                                    off_base[:, bass.ds(d, 1)], None, ALU.subtract).then_inc(s_rel, 1)
                for q in range(QUADS):
                    e.wait_ge(s_nodes, QUADS * c + q + 1)
                    e.wait_ge(s_quad, QUADS * c + q + 4)
                    own = cols_f[n][:, bass.ds(d, 1), QUAD * q:QUAD * (q + 1)].rearrange(
                        "p a (j k) -> p (a j) k", k=1).to_broadcast([P, QUAD, P])
                    e.tensor_tensor(same[q % 2][:, :, :],
                                    ps_nodes[q % 2][:, :].rearrange("p (j k) -> p j k", k=P),
                                    own, ALU.is_equal).then_inc(s_same, 1)
                    if window:
                        if q == 0:
                            e.wait_ge(s_rel, c + 1)
                        for j in range(QUAD):
                            hot = e.tensor_scalar(onehot[q % 2][:, j, :], iota, rel[b][:, QUAD * q + j:QUAD * q + j + 1],
                                                  None, ALU.is_equal)
                        hot.then_inc(s_hot, 1)
                e.wait_ge(s_ev, QUADS * c + QUADS + 2)
                e.wait_ge(s_free, 2 * c + 2)
                e.tensor_scalar(repeated[:, :], payload[b][:, :, D], unweight, 2.5, ALU.mult, ALU.is_ge).then_inc(s_rep, 1)
                if window:
                    e.tensor_copy(win_now[b][:, :], win_rows[:, bass.ds(d, 1)]).then_inc(s_rep, 1)
                e.wait_ge(s_rep, (2 * c + 2) if window else (N_CHUNKS + c + 1))
                e.scalar_tensor_tensor(target[b][:, :], repeated[:, :], spare_row[:, 0:1],
                                       cols_f[n][:, bass.ds(d, 1), :].rearrange("p a j -> p (a j)"),
                                       ALU.mult, ALU.max).then_inc(s_tgt, 1)

            def pad(c):
                e.wait_ge(s_quad, QUADS * c + 1)
                e.memset(feat[1][64:P, :, :], 0.0).then_inc(s_pad, 1)

            def all_chunks(offset, n, window):
                with e.Fori(offset, offset + PAIRS - 1) as i:
                    for b in range(2):
                        chunk(2 * i + b, b, 2 * (i - offset) + b, n, window)
                c = 2 * (offset + PAIRS - 1)
                pad(c + 1)
                for b in range(2):
                    chunk(c + b, b, N_CHUNKS - 2 + b, n, window)

            all_chunks(0, 0, True)
            again = e.value_load(flag_i[0:1, 0:1], min_val=0, max_val=1)
            with e.If(again > 0):
                all_chunks(PAIRS, 1, False)

            for s in range(NSEG + 1):
                b, n = s % 2, SEG if s < NSEG else 1
                e.wait_ge(s_seg[b], 16 * (OUT_TABLES + 1) * (s // 2 + 1))
                half = n * D // 2
                to = agg_out[:, s * SEG:s * SEG + n, :].rearrange("p r d -> p (r d)")
                for h in range(2):
                    e.tensor_reduce(to[:, h * half:(h + 1) * half],
                                    tabs[b][:, :, h * half:(h + 1) * half].rearrange("p k f -> p f k"),
                                    AX.X, ALU.add).then_inc(s_sum, 1)
                if s == 0:
                    e.wait_ge(s_x, 32)
                    e.wait_ge(s_w, 80)
                    e.tensor_tensor(y[:, :, :], xs[:, :, :],
                                    b2s[:, :].rearrange("p (a d) -> p a d", a=1).to_broadcast([P, N_TILES, D]),
                                    ALU.add).then_inc(s_xb, 1)
                    e.wait_ge(s_xb, 1)
                done = N_TILES if s == NSEG else (s + 1) * SEG
                before = s * SEG
                for g, (a, z) in enumerate(GROUPS):
                    if before < z <= done:
                        node_group(e, g, a, z)

        @block.tensor
        def _(e):
            e.wait_ge(s_one, 3)
            for w, (n, a, z) in enumerate(TBATCH):
                if a == 0:
                    e.wait_ge(s_pre, 2 + 2 * n)
                if w >= 4:
                    e.wait_ge(s_te, w - 3)
                for j in range(a, z):
                    last = e.transpose(bank[w % 4][:, (j - a) * N_CHUNKS:(j - a + 1) * N_CHUNKS],
                                       rows_f[:, j::COLS], ident[0:N_CHUNKS, 0:N_CHUNKS])
                last.then_inc(s_tp, 1)
            e.wait_ge(s_pre, 10)
            e.matmul(bank[4][:, 0:N_CHUNKS], ones[0:N_CHUNKS, :], diag[:, :], start=True, stop=True)
            e.matmul(bank[5][:, 0:1], ones[0:N_CHUNKS, :], wide[:, :], start=True, stop=True).then_inc(s_b, 1)
            e.wait_ge(s_te, len(TBATCH))
            e.wait_ge(s_pre, PRE_FLAG)

            def spread(d, q, n):
                row = ident_bf[0:N_CHUNKS, bass.ds(d, 1)].to_broadcast([N_CHUNKS, P])
                for k, part in enumerate((rows_hi[n], rows_lo[n])):
                    v = part[:, :].rearrange("c (p q j) -> c q j p", q=QUADS, j=QUAD)
                    last = e.matmul(ps_nodes[q % 2][:, :], row, v[:, q, :, :], start=(k == 0), stop=(k == 1))
                last.then_inc(s_nodes, 1)

            def chunk(i, c, b, d, n, window):
                spread(d, 0, n)
                spread(d, 1, n)
                e.wait_ge(s_feat[b], 16 * (i + 1))
                if window:
                    e.wait_ge(s_wev, c + 1)
                for q in range(QUADS):
                    e.wait_ge(s_same, QUADS * c + q + 1)
                    e.wait_ge(s_ev, QUADS * c + q + 1)
                    for j in range(QUAD):
                        t = QUAD * q + j
                        o = j * (D + 1)
                        e.matmul(ps_pay[q % 2][:, o:o + D], same[q % 2][:, j, :], feat[b][:, t, :],
                                 start=True, stop=True)
                        last = e.matmul(ps_pay[q % 2][:, o + D:o + D + 1], same[q % 2][:, j, :], weight,
                                        start=True, stop=True)
                    last.then_inc(s_pay, 1)
                    if q + 2 < QUADS:
                        spread(d, q + 2, n)
                    if window:
                        e.wait_ge(s_hot, QUADS * c + q + 1)
                        for j in range(QUAD):
                            t = QUAD * q + j
                            last = e.matmul(ps_win[b][:, 0:D], onehot[q % 2][:, j, :], feat[b][:, t, :],
                                            start=(t == 0), stop=(t == COLS - 1))
                        last.then_inc(s_quad, 1)
                    else:
                        e.drain().then_inc(s_quad, 1)

            e.wait_ge(s_rows, 2)
            with e.Fori(0, PAIRS) as i:
                for b in range(2):
                    chunk(i, 2 * i + b, b, 2 * i + b, 0, True)
            again = e.value_load(flag_i[0:1, 0:1], min_val=0, max_val=1)
            with e.If(again > 0):
                with e.Fori(PAIRS, 2 * PAIRS) as i:
                    for b in range(2):
                        chunk(i, 2 * i + b, b, 2 * i + b - N_CHUNKS, 1, False)

            e.wait_ge(s_agg, 1)
            e.wait_ge(s_x, 32)
            e.wait_ge(s_w, 80)
            for g, (a, z) in enumerate(GROUPS):
                n = P * (z - a)
                seg = min((z - 1) // SEG, NSEG)
                e.wait_ge(s_sum, 2 * (seg + 1))
                e.wait_ge(s_seg[seg % 2], 16 * (OUT_TABLES + 1) * (seg // 2 + 1))
                if g:
                    e.wait_ge(s_nte, g)
                for t in range(a, z):
                    o = P * (t - a)
                    e.transpose(bank[0][0:D, o:o + P], agg_in[:, t, :], ident)
                    e.matmul(bank[0][D:2 * D, o:o + P], agg_out[:, t, :], ident, start=True, stop=True)
                    last = e.transpose(bank[1][0:D, o:o + P], xs[:, t, :], ident)
                last.then_inc(s_nt, 1)
                e.wait_ge(s_nte, g + 1)
                for m in range(2):
                    if g:
                        e.wait_ge(s_hr, 2 * (g - 1) + m + 1)
                    e.matmul(bank[2 + m][:, 0:n], w1io[:, m * P:(m + 1) * P], catT[:, 0:n], start=True, stop=False)
                    e.matmul(bank[2 + m][:, 0:n], w1x[:, m * P:(m + 1) * P], xT[:, 0:n],
                             start=False, stop=True).then_inc(s_h, 1)
                e.wait_ge(s_hr, 2 * g + 2)
                if g:
                    e.wait_ge(s_y, g)
                for t in range(a, z):
                    o = P * (t - a)
                    for m in range(2):
                        last = e.matmul(bank[4][:, (t - a) * D:(t - a + 1) * D], hid[:, m, o:o + P], w2s[:, m, :],
                                        start=(m == 0), stop=(m == 1))
                last.then_inc(s_o, 1)


def kernel(x, src, dst, edge_attr_64, L0_gnn_W1, L0_gnn_b1, L0_gnn_W2, L0_gnn_b2):
    import numpy as np
    from concourse import bacc
    from concourse.bass_utils import run_bass_kernel_spmd

    part = np.arange(P, dtype=np.float32)[:, None]
    consts = np.concatenate([np.eye(P, dtype=np.float32), np.tile(part.T, (P, 1)),
                             np.exp2(POW - part), np.exp2(part - POW), part], axis=1).astype(np.float32)
    inputs = {"x": x, "src": src, "dst": dst, "edge_attr": edge_attr_64, "w1": L0_gnn_W1, "b1": L0_gnn_b1,
              "w2": L0_gnn_W2, "b2": L0_gnn_b2, "consts": consts}
    arrays = {f"in_{k}": np.ascontiguousarray(v) for k, v in inputs.items()}
    nc = bacc.Bacc("TRN2", target_bir_lowering=False, num_devices=1)
    args = [nc.dram_tensor(k, v.shape, mybir.dt.from_np(v.dtype), kind="ExternalInput").ap()
            for k, v in arrays.items()]
    out = nc.dram_tensor("out", (N_NODES, D), mybir.dt.float32, kind="ExternalOutput").ap()
    build(nc, *args, out)
    r = run_bass_kernel_spmd(nc, [arrays], core_ids=[0])
    return r.results[0]["out"]
```

```python
from contextlib import ExitStack

import concourse.bass as bass
from concourse import mybir
from concourse.alu_op_type import AluOpType as ALU

N_NODES = 6250
N_EDGES = 200000
D = 64
D_HID = 256
P = 128
EPS = 1e-05

COLS = 16
QUAD = 4
QUADS = COLS // QUAD
CHUNK = P * COLS
N_CHUNKS = -(-N_EDGES // CHUNK)
LAST_EDGES = N_EDGES - (N_CHUNKS - 1) * CHUNK
LAST_PARTS = LAST_EDGES // COLS
PAD = CHUNK - LAST_EDGES
PAIRS = N_CHUNKS // 2
assert N_CHUNKS % 2 == 0 and LAST_EDGES % COLS == 0 and PAD <= LAST_EDGES

OUT_TABLES = 8
TABLE_ROWS = 6400
SPARE = N_NODES
ZERO_TIMES = 5
assert TABLE_ROWS >= N_NODES + P and TABLE_ROWS % P == 0

NT = N_NODES // P
N_TILES = NT + 1
REST = N_NODES - NT * P
GT = 4
assert NT % (2 * GT) == 0
POW = 60


def build(nc, x, src, dst, edges, w1, b1, w2, b2, consts, out):
    fp32 = mybir.dt.float32
    bf16 = mybir.dt.bfloat16
    i32 = mybir.dt.int32
    ACT = mybir.ActivationFunctionType
    AX = mybir.AxisListType

    out_tab = nc.dram_tensor("out_tables", (OUT_TABLES * TABLE_ROWS, D), fp32, kind="Internal").ap()
    in_tab = nc.dram_tensor("in_table", (TABLE_ROWS, D), fp32, kind="Internal").ap()

    with ExitStack() as ctx:
        def sb(name, shape, dt=fp32):
            return ctx.enter_context(nc.sbuf_tensor(name, shape, dt))

        def ps(name, shape):
            return ctx.enter_context(nc.psum_tensor(name, shape, fp32))

        def sem(name):
            return ctx.enter_context(nc.semaphore(name))

        cst = sb("cst", [P, 2 * P + 3])
        ident = cst[:, 0:P]
        iota = cst[:, P:2 * P]
        weight = cst[:, 2 * P:2 * P + 1]
        unweight = cst[:, 2 * P + 1:2 * P + 2]
        part_no = cst[:, 2 * P + 2:2 * P + 3]
        spare_row = sb("spare_row", [P, 1])
        ident_bf = sb("ident_bf", [P, P], bf16)
        ones = sb("ones", [P, P])
        zeros = sb("zeros", [P, 1, TABLE_ROWS // P // ZERO_TIMES * D])

        rows_i = [sb(f"rows_i{n}", [N_CHUNKS, CHUNK], i32) for n in range(2)]
        part_i = sb("part_i", [N_CHUNKS, CHUNK], i32)
        rows_f = sb("rows_f", [N_CHUNKS, CHUNK])
        rows_hi = [sb(f"rows_hi{n}", [N_CHUNKS, CHUNK], bf16) for n in range(2)]
        rows_lo = [sb(f"rows_lo{n}", [N_CHUNKS, CHUNK], bf16) for n in range(2)]
        cols_f = [sb(f"cols_f{n}", [P, N_CHUNKS, COLS]) for n in range(2)]
        lowest = sb("lowest", [N_CHUNKS, 1])
        highest = sb("highest", [N_CHUNKS, 1])
        wide = sb("wide", [N_CHUNKS, 1])
        diag = sb("diag", [N_CHUNKS, N_CHUNKS])
        base = sb("base", [P, N_CHUNKS])
        off_base = sb("off_base", [P, N_CHUNKS])
        win_rows = sb("win_rows", [P, N_CHUNKS], i32)
        shift = sb("shift", [P, 1])
        flag_i = sb("flag_i", [P, 1], i32)

        feat = [sb(f"feat{b}", [P, COLS, D]) for b in range(2)]
        rest = [sb(f"rest{b}", [P, COLS, D]) for b in range(2)]
        parts = [sb(f"parts{b}", [P, COLS, 1 + 3 * D], bf16) for b in range(2)]
        iota_bf = sb("iota_bf", [P, P], bf16)
        same = [sb(f"same{b}", [P, QUAD, P], bf16) for b in range(2)]
        onehot = [sb(f"onehot{b}", [P, QUAD, P], bf16) for b in range(2)]
        rel = [sb(f"rel{b}", [P, COLS]) for b in range(2)]
        payload = [sb(f"payload{b}", [P, COLS, D]) for b in range(2)]
        weights = [sb(f"weights{b}", [P, COLS]) for b in range(2)]
        win_pay = [sb(f"win_pay{b}", [P, D]) for b in range(2)]
        repeated = sb("repeated", [P, COLS])
        target = [sb(f"target{b}", [P, COLS], i32) for b in range(2)]

        w1io = sb("w1io", [P, D_HID])
        w1x = sb("w1x", [D, D_HID])
        w2s = sb("w2s", [P, 2, 2 * D])
        b1s = sb("b1s", [P, 2])
        b2s = sb("b2s", [P, D])
        xs = sb("xs", [P, N_TILES, D])

        bank = [ps(f"bank{n}", [P, 512]) for n in range(8)]
        ps_nodes = bank[0:2]
        ps_pay = bank[2:4]
        ps_win = bank[4:6]

        s_cst = sem("s_cst")
        s_row = [sem(f"s_row{n}") for n in range(2)]
        s_w = sem("s_w")
        s_x = sem("s_x")
        s_xz = sem("s_xz")
        s_one = sem("s_one")
        s_zero = sem("s_zero")
        s_pad = sem("s_pad")
        s_pre = sem("s_pre")
        s_tp = sem("s_tp")
        s_te = sem("s_te")
        s_b = sem("s_b")
        s_rows = sem("s_rows")
        s_feat = [sem(f"s_feat{b}") for b in range(2)]
        s_hi = sem("s_hi")
        s_rest = sem("s_rest")
        s_mid = sem("s_mid")
        s_lo = sem("s_lo")
        s_nodes = sem("s_nodes")
        s_same = sem("s_same")
        s_hot = sem("s_hot")
        s_rel = sem("s_rel")
        s_pay = sem("s_pay")
        s_quad = sem("s_quad")
        s_ev = sem("s_ev")
        s_wev = sem("s_wev")
        s_rep = sem("s_rep")
        s_tgt = sem("s_tgt")
        s_free = sem("s_free")
        s_tab = [sem(f"s_tab{k}") for k in range(OUT_TABLES)]
        s_in = sem("s_in")
        s_agg = sem("s_agg")

        GROUPS = NT // GT
        tabs = [sb(f"tabs{b}", [P, OUT_TABLES, GT * D]) for b in range(2)]
        agg = [sb(f"agg{b}", [P, GT, 2 * D]) for b in range(2)]
        catT = [sb(f"catT{b}", [2 * D, GT * P]) for b in range(2)]
        xT = [sb(f"xT{b}", [D, GT * P]) for b in range(2)]
        x_now = [sb(f"x_now{b}", [P, GT, D]) for b in range(2)]
        y = sb("y", [P, GT, D])
        y_sum = sb("y_sum", [P, GT, D])
        hid = sb("hid", [P, 2, GT * P])
        stats = sb("stats", [P, GT, 6])
        mv = sb("mv", [P, GT, 2])
        sd = sb("sd", [P, GT])
        rstd = sb("rstd", [P, GT])
        s_load = [sem(f"s_load{b}") for b in range(2)]
        s_sum = sem("s_sum")
        s_xg = sem("s_xg")
        s_nt = sem("s_nt")
        s_cat = sem("s_cat")
        s_h = sem("s_h")
        s_relu = sem("s_relu")
        s_o = sem("s_o")
        s_y = sem("s_y")
        s_yb = sem("s_yb")
        s_st = sem("s_st")
        s_ag = sem("s_ag")
        s_sd = sem("s_sd")
        s_rs = sem("s_rs")
        s_ln = sem("s_ln")
        s_out = sem("s_out")
        win_now = [sb(f"win_now{b}", [P, 1], i32) for b in range(2)]
        eps = sb("eps", [P, 1])
        PRE_FLAG = 13
        W_LOADS = 5
        block = ctx.enter_context(nc.Block())

        row_view = [v[0:(N_CHUNKS - 1) * CHUNK].rearrange("(c k) -> c k", k=CHUNK) for v in (src, dst)]
        TB = 5
        TBATCH = [(n, a, min(a + TB, COLS)) for n in range(2) for a in range(0, COLS, TB)]

        def tiles_of(t, g, lead=0):
            if isinstance(g, int) and g == GROUPS:
                return t[lead + NT * P:lead + (NT + 1) * P, :]
            rows = t[lead:lead + NT * P, :].rearrange("(p r) d -> p (r d)", r=NT)
            return rows[:, bass.ds(g * (GT * D), GT * D)]

        def tiles_in(g):
            return 1 if isinstance(g, int) and g == GROUPS else GT

        def tile_cols(t, g, n):
            return t[:, bass.ds(g * GT, n), :]

        def all_groups(e, group):
            with e.Fori(0, GROUPS // 2 - 1) as j:
                for b in range(2):
                    group(j, 2 * j + b, b)
            for g in range(GROUPS - 2, GROUPS + 1):
                group(g // 2, g, g % 2)

        @block.sync
        def _(e):
            e.dma_start(cst[:, :], consts).then_inc(s_cst, 16)
            for n, v in enumerate((src, dst)):
                full = (N_CHUNKS - 1) // 16 * 16
                e.dma_start(rows_i[n][0:full, :], row_view[n][0:full, :]).then_inc(s_row[n], 16)
                e.dma_start(rows_i[n][full:N_CHUNKS - 1, :], row_view[n][full:, :]).then_inc(s_row[n], 16)
                last = v[(N_CHUNKS - 1) * CHUNK:N_EDGES].rearrange("(a k) -> a k", a=1)
                e.dma_start(rows_i[n][N_CHUNKS - 1:N_CHUNKS, 0:LAST_EDGES], last).then_inc(s_row[n], 16)
                e.dma_start(rows_i[n][N_CHUNKS - 1:N_CHUNKS, LAST_EDGES:CHUNK],
                            last[:, LAST_EDGES - PAD:LAST_EDGES]).then_inc(s_row[n], 16)

            def load_chunks(pair, first_chunk, last_pair):
                for b in range(2):
                    c = first_chunk + b
                    e.wait_ge(s_rest, c + 1)
                    if last_pair and b == 1:
                        e.wait_ge(s_pad, 1 if first_chunk == N_CHUNKS - 2 else 2)
                        e.dma_start(feat[b][0:LAST_PARTS, :, :],
                                    edges[(N_CHUNKS - 1) * CHUNK:N_EDGES, :].rearrange(
                                        "(p j) d -> p j d", j=COLS)).then_inc(s_feat[b], 16)
                    else:
                        at = (2 * pair + b) * CHUNK
                        e.dma_start(feat[b][:, :, :],
                                    edges[bass.ds(at, CHUNK), :].rearrange(
                                        "(p j) d -> p j d", j=COLS)).then_inc(s_feat[b], 16)

            def all_chunks(offset):
                with e.Fori(offset, offset + PAIRS - 1) as i:
                    load_chunks(i - offset, 2 * i, False)
                load_chunks(PAIRS - 1, 2 * (offset + PAIRS - 1), True)

            all_chunks(0)
            e.wait_ge(s_pre, PRE_FLAG)
            again = e.value_load(flag_i[0:1, 0:1], min_val=0, max_val=1)
            with e.If(again > 0):
                all_chunks(PAIRS)

            def load_group(g, b):
                n = tiles_in(g)
                for k in range(OUT_TABLES):
                    e.dma_start(tabs[b][:, k, 0:n * D], tiles_of(out_tab, g, k * TABLE_ROWS)).then_inc(s_load[b], 16)
                e.dma_start(agg[b][:, 0:n, 0:D],
                            tiles_of(in_tab, g).rearrange("p (r d) -> p r d", d=D)).then_inc(s_load[b], 16)

            def group(j, g, b):
                if not isinstance(g, int) or g + 2 <= GROUPS:
                    e.wait_ge(s_sum, g + 1)
                    e.wait_ge(s_nt, g + 1)
                    load_group(g + 2, b)
                e.wait_ge(s_ln, g + 1)
                if isinstance(g, int) and g == GROUPS:
                    e.dma_start(out[NT * P:N_NODES, :], xs[0:REST, NT, :]).then_inc(s_out, 16)
                else:
                    e.dma_start(tiles_of(out, g), tile_cols(xs, g, GT).rearrange("p r d -> p (r d)")).then_inc(s_out, 16)

            e.wait_ge(s_agg, 1)
            load_group(0, 0)
            load_group(1, 1)
            all_groups(e, group)
            e.wait_ge(s_out, 16 * (GROUPS + 1))

        @block.gpsimd
        def _(e):
            e.sem_inc(s_free, 3)
            e.wait_ge(s_zero, 1)
            for k in range(OUT_TABLES + 1):
                table = out_tab[k * TABLE_ROWS:(k + 1) * TABLE_ROWS, :] if k < OUT_TABLES else in_tab
                e.dma_start(table.rearrange("(p t r) d -> p t (r d)", p=P, t=ZERO_TIMES),
                            zeros[:, :, :].to_broadcast([P, ZERO_TIMES, zeros.shape[2]])
                            ).then_inc(s_tab[k] if k < OUT_TABLES else s_in, 16)

            def add_chunk(c, b, d, window):
                e.wait_ge(s_tgt, c + 1)
                for t in range(COLS):
                    if t % QUAD == 0:
                        e.wait_ge(s_ev, QUADS * c + t // QUAD + 3)
                    at = bass.IndirectOffsetOnAxis(ap=target[b][:, t:t + 1], axis=0)
                    if window:
                        k, turn = t % OUT_TABLES, COLS // OUT_TABLES * c + t // OUT_TABLES
                        e.wait_ge(s_tab[k], 16 * turn + 16)
                        e.nop(nofuse=True)
                        e.indirect_dma_start(out_tab, at, payload[b][:, t, :], None,
                                             element_offset=k * TABLE_ROWS * D, compute_op=ALU.add).then_inc(s_tab[k], 16)
                    else:
                        e.wait_ge(s_in, 16 * (COLS * (c - N_CHUNKS) + t + N_CHUNKS + 1))
                        e.nop(nofuse=True)
                        e.indirect_dma_start(in_tab, at, payload[b][:, t, :], None,
                                             compute_op=ALU.add).then_inc(s_in, 16)
                    if t == COLS // 2 - 2:
                        if window:
                            e.wait_ge(s_wev, c + 3)
                            e.wait_ge(s_in, 16 * c + 16)
                            e.nop(nofuse=True)
                            e.indirect_dma_start(
                                in_tab, bass.IndirectOffsetOnAxis(ap=win_now[b][:, 0:1], axis=0),
                                win_pay[b][:, :], None, compute_op=ALU.add).then_inc(s_in, 16)
                    if t % (COLS // 2) == COLS // 2 - 1:
                        e.sem_inc(s_free, 1)

            with e.Fori(0, PAIRS) as i:
                for b in range(2):
                    add_chunk(2 * i + b, b, 2 * i + b, True)
            e.wait_ge(s_pre, PRE_FLAG)
            again = e.value_load(flag_i[0:1, 0:1], min_val=0, max_val=1)
            with e.If(again > 0):
                with e.Fori(PAIRS, 2 * PAIRS) as i:
                    for b in range(2):
                        add_chunk(2 * i + b, b, 2 * i + b - N_CHUNKS, False)
                e.wait_ge(s_in, 16 * (COLS * N_CHUNKS + N_CHUNKS + 1))
            for k in range(OUT_TABLES):
                e.wait_ge(s_tab[k], 16 * (COLS * N_CHUNKS // OUT_TABLES + 1))
            e.wait_ge(s_in, 16 * (N_CHUNKS + 1))
            e.sem_inc(s_agg, 1)

        @block.scalar
        def _(e):
            e.dma_start(w1io[:, :], w1[0:2 * D, :]).then_inc(s_w, 16)
            e.dma_start(w1x[:, :], w1[2 * D:3 * D, :]).then_inc(s_w, 16)
            e.dma_start(w2s[:, :, 0:D], w2.rearrange("(a p) n -> p a n", p=P)).then_inc(s_w, 16)
            with nc.allow_non_contiguous_dma(reason="256 biases, once"):
                e.dma_start(b1s[:, :], b1.rearrange("(a p) -> p a", p=P)).then_inc(s_w, 16)
            e.dma_start(b2s[:, :], b2.rearrange("(a n) -> a n", a=1).to_broadcast([P, D])).then_inc(s_w, 16)
            e.wait_ge(s_xz, 1)
            e.dma_start(xs[:, 0:NT, :].rearrange("p r d -> p (r d)"),
                        x[0:NT * P, :].rearrange("(p r) d -> p (r d)", r=NT)).then_inc(s_x, 16)
            e.dma_start(xs[0:REST, NT, :], x[NT * P:, :]).then_inc(s_x, 16)

            e.sem_inc(s_ev, 2)

            def split_hi(i, c, b):
                e.wait_ge(s_feat[b], 16 * (i + 1))
                e.wait_ge(s_quad, QUADS * c + 1)
                e.activation(parts[b][:, :, 1:1 + D], feat[b][:, :, :], ACT.Copy).then_inc(s_hi, 1)

            def split_mid(c, b):
                e.wait_ge(s_rest, c + 3)
                e.activation(parts[b][:, :, 1 + D:1 + 2 * D], rest[b][:, :, :], ACT.Copy).then_inc(s_mid, 1)

            def chunk(i, c, b, ahead):
                if ahead:
                    split_hi(i + b, c + 1, 1 - b)
                for q in range(QUADS):
                    if q % 2 == 0:
                        e.wait_ge(s_free, 2 * c + q // 2 + 1)
                    e.wait_ge(s_pay, QUADS * c + q + 1)
                    quad = ps_pay[q % 2][:, 0:QUAD * (D + 1)].rearrange("p (t d) -> p t d", d=D + 1)
                    e.activation(payload[b][:, QUAD * q:QUAD * (q + 1), :], quad[:, :, 1:D + 1], ACT.Copy)
                    e.activation(weights[b][:, QUAD * q:QUAD * (q + 1)], quad[:, :, 0], ACT.Copy).then_inc(s_ev, 1)
                    if ahead and q == 0:
                        split_mid(c + 1, 1 - b)

            def all_chunks(offset):
                split_hi(offset, 2 * offset, 0)
                split_mid(2 * offset, 0)
                with e.Fori(offset, offset + PAIRS - 1) as i:
                    for b in range(2):
                        chunk(i, 2 * i + b, b, True)
                i = offset + PAIRS - 1
                for b in range(2):
                    chunk(i, 2 * i + b, b, b == 0)

            all_chunks(0)
            e.wait_ge(s_pre, PRE_FLAG)
            again = e.value_load(flag_i[0:1, 0:1], min_val=0, max_val=1)
            with e.If(again > 0):
                all_chunks(PAIRS)

            def out_of_transposes(g, b):
                n = tiles_in(g) * P
                e.wait_ge(s_nt, g + 1)
                e.activation(catT[b][:, 0:n], bank[b][:, 0:n], ACT.Copy)
                e.activation(xT[b][:, 0:n], bank[2 + b][0:D, 0:n], ACT.Copy).then_inc(s_cat, 1)

            def group(j, g, b):
                n = tiles_in(g) * P
                e.wait_ge(s_o, g + 1)
                for m in range(2):
                    e.wait_ge(s_h, 2 * g + m + 1)
                    e.activation(hid[:, m, 0:n], bank[4 + m][:, 0:n], ACT.Relu,
                                 bias=b1s[:, m:m + 1]).then_inc(s_relu, 1)
                if not isinstance(g, int) or g < GROUPS:
                    out_of_transposes(g + 1, 1 - b)
                e.wait_ge(s_ag, g + 1)
                e.activation(sd[:, 0:tiles_in(g)], mv[:, 0:tiles_in(g), 1], ACT.Sqrt, bias=eps[:, 0:1]).then_inc(s_sd, 1)

            e.wait_ge(s_w, 16 * W_LOADS)
            out_of_transposes(0, 0)
            all_groups(e, group)

        @block.vector
        def _(e):
            steps = [0]

            def step(ins):
                steps[0] += 1
                ins.then_inc(s_pre, 1)
                e.wait_ge(s_pre, steps[0])

            e.memset(zeros[:, :, :], 0.0).then_inc(s_zero, 1)
            e.memset(ones[:, :], 1.0).then_inc(s_one, 1)
            e.memset(eps[:, :], EPS).then_inc(s_one, 1)
            e.memset(xs[96:P, NT, :], 0.0).then_inc(s_xz, 1)
            for s, first in ((s_wev, 2), (s_rest, 2), (s_y, 2), (s_o, 1)):
                e.sem_inc(s, first)
            e.memset(w2s[:, :, D:2 * D], 0.0).then_inc(s_one, 1)
            e.sem_inc(s_quad, QUADS + 1)
            e.wait_ge(s_cst, 16)
            e.tensor_copy(ident_bf[:, :], ident).then_inc(s_one, 1)
            e.tensor_copy(iota_bf[:, :], iota)
            for b in range(2):
                e.tensor_copy(parts[b][:, :, 0], weight.to_broadcast([P, COLS])).then_inc(s_one, 1)
            step(e.tensor_scalar(spare_row[:, :], part_no, float(SPARE), None, ALU.add))
            for n in range(2):
                e.wait_ge(s_row[n], 64)
                if n == 1:
                    e.wait_ge(s_tp, 4)
                step(e.tensor_copy(rows_f[:, :], rows_i[n][:, :]))
                step(e.tensor_scalar(part_i[:, :], rows_i[n][:, :], 0x1F80, None, ALU.bitwise_and))
                e.tensor_copy(rows_hi[n][:, :], part_i[:, :])
                e.tensor_tensor(rows_lo[n][:, :], rows_i[n][:, :], part_i[:, :], ALU.subtract).then_inc(s_rows, 1)
                for w, (nn, a, z) in enumerate(TBATCH):
                    if nn == n:
                        e.wait_ge(s_tp, w + 1)
                        e.tensor_copy(cols_f[n][:, :, a:z].rearrange("p c j -> p j c"),
                                      bank[w % 4][:, 0:(z - a) * N_CHUNKS].rearrange(
                                          "p (j c) -> p j c", c=N_CHUNKS)).then_inc(s_te, 1)
                e.wait_ge(s_te, 4 * (n + 1))
                e.wait_ge(s_rows, n + 1)
            step(e.tensor_reduce(lowest[:, :], rows_f[:, :], AX.X, ALU.min))
            step(e.tensor_reduce(highest[:, :], rows_f[:, :], AX.X, ALU.max))
            step(e.tensor_tensor(wide[:, :], highest[:, :], lowest[:, :], ALU.subtract))
            step(e.tensor_scalar(wide[:, :], wide[:, :], P - 0.5, None, ALU.is_gt))
            step(e.tensor_scalar(diag[:, :], ident[0:N_CHUNKS, 0:N_CHUNKS], lowest[:, 0:1], None, ALU.mult))
            e.wait_ge(s_b, 1)
            step(e.tensor_copy(base[:, :], bank[4][:, 0:N_CHUNKS]))
            step(e.tensor_scalar(shift[:, :], bank[5][:, 0:1], 0.5, None, ALU.is_gt))
            step(e.tensor_copy(flag_i[:, :], shift[:, :]))
            assert steps[0] == PRE_FLAG
            step(e.tensor_scalar(shift[:, :], shift[:, :], float(1 << 14), None, ALU.mult))
            step(e.tensor_scalar(off_base[:, :], base[:, :], shift[:, 0:1], None, ALU.subtract))
            step(e.tensor_scalar(win_rows[:, :], base[:, :], part_no, None, ALU.add))

            def split_rest(c, b):
                e.wait_ge(s_hi, c + 1)
                e.tensor_tensor(rest[b][:, :, :], feat[b][:, :, :], parts[b][:, :, 1:1 + D],
                                ALU.subtract).then_inc(s_rest, 1)

            def split_lo(c, b):
                e.wait_ge(s_mid, c + 1)
                e.tensor_tensor(parts[b][:, :, 1 + 2 * D:1 + 3 * D], rest[b][:, :, :],
                                parts[b][:, :, 1 + D:1 + 2 * D], ALU.subtract).then_inc(s_lo, 1)

            def chunk(c, b, d, n, window, ahead):
                if window:
                    e.wait_ge(s_quad, QUADS * c + 1)
                    e.tensor_scalar(rel[b][:, :], cols_f[1][:, bass.ds(d, 1), :].rearrange("p a j -> p (a j)"),
                                    off_base[:, bass.ds(d, 1)], None, ALU.subtract).then_inc(s_rel, 1)
                for q in range(QUADS):
                    e.wait_ge(s_nodes, QUADS * c + q + 1)
                    e.wait_ge(s_quad, QUADS * c + q + 4)
                    own = cols_f[n][:, bass.ds(d, 1), QUAD * q:QUAD * (q + 1)].rearrange(
                        "p a (j k) -> p (a j) k", k=1).to_broadcast([P, QUAD, P])
                    e.tensor_tensor(same[q % 2][:, :, :],
                                    ps_nodes[q % 2][:, :].rearrange("p (j k) -> p j k", k=P),
                                    own, ALU.is_equal).then_inc(s_same, 1)
                    if window:
                        if q == 0:
                            e.wait_ge(s_rel, c + 1)
                        for j in range(QUAD):
                            hot = e.tensor_scalar(onehot[q % 2][:, j, :], iota_bf[:, :],
                                                  rel[b][:, QUAD * q + j:QUAD * q + j + 1], None, ALU.is_equal)
                        hot.then_inc(s_hot, 1)
                    if ahead and q == 0:
                        split_rest(c + 1, 1 - b)
                    if ahead and q == 2:
                        split_lo(c + 1, 1 - b)
                e.wait_ge(s_ev, QUADS * c + QUADS + 2)
                e.wait_ge(s_free, 2 * c + 2)
                e.tensor_scalar(repeated[:, :], weights[b][:, :], unweight, 2.5, ALU.mult, ALU.is_ge).then_inc(s_rep, 1)
                if window:
                    e.tensor_copy(win_now[b][:, :], win_rows[:, bass.ds(d, 1)]).then_inc(s_rep, 1)
                e.wait_ge(s_rep, (2 * c + 2) if window else (N_CHUNKS + c + 1))
                e.scalar_tensor_tensor(target[b][:, :], repeated[:, :], spare_row[:, 0:1],
                                       cols_f[n][:, bass.ds(d, 1), :].rearrange("p a j -> p (a j)"),
                                       ALU.mult, ALU.max).then_inc(s_tgt, 1)
                if window:
                    e.wait_ge(s_quad, QUADS * c + 9)
                    e.tensor_reduce(win_pay[b][:, :], ps_win[b][:, 0:3 * D].rearrange("p (k d) -> p d k", k=3),
                                    AX.X, ALU.add).then_inc(s_wev, 1)

            def pad(c):
                e.wait_ge(s_rest, c + 1)
                e.memset(feat[1][64:P, :, :], 0.0).then_inc(s_pad, 1)

            def all_chunks(offset, n, window):
                split_rest(2 * offset, 0)
                split_lo(2 * offset, 0)
                with e.Fori(offset, offset + PAIRS - 1) as i:
                    for b in range(2):
                        chunk(2 * i + b, b, 2 * (i - offset) + b, n, window, True)
                c = 2 * (offset + PAIRS - 1)
                pad(c + 1)
                for b in range(2):
                    chunk(c + b, b, N_CHUNKS - 2 + b, n, window, b == 0)

            all_chunks(0, 0, True)
            again = e.value_load(flag_i[0:1, 0:1], min_val=0, max_val=1)
            with e.If(again > 0):
                all_chunks(PAIRS, 1, False)

            def sum_tables(j, g, b):
                n = tiles_in(g)
                e.tensor_copy(x_now[b][:, 0:n, :], tile_cols(xs, g, n)).then_inc(s_xg, 1)
                e.wait_ge(s_load[b], 16 * (OUT_TABLES + 1) * (j + 1))
                e.tensor_reduce(agg[b][:, 0:n, D:2 * D],
                                tabs[b][:, :, 0:n * D].rearrange("p k (r d) -> p r d k", d=D),
                                AX.X, ALU.add).then_inc(s_sum, 1)

            def group(j, g, b):
                n = tiles_in(g)
                if not isinstance(g, int) or g < GROUPS:
                    sum_tables(j + b, g + 1, 1 - b)
                e.wait_ge(s_o, g + 2)
                e.tensor_tensor(y_sum[:, 0:n, :], x_now[b][:, 0:n, :],
                                bank[6 + b][:, 0:n * P].rearrange("p (t d) -> p t d", d=P)[:, :, 0:D],
                                ALU.add).then_inc(s_y, 1)
                e.wait_ge(s_y, g + 3)
                e.tensor_tensor(y[:, 0:n, :], y_sum[:, 0:n, :],
                                b2s[:, :].rearrange("p (a d) -> p a d", a=1).to_broadcast([P, n, D]),
                                ALU.add).then_inc(s_yb, 1)
                e.wait_ge(s_yb, g + 1)
                for t in range(n):
                    last = e.bn_stats(stats[:, t, :], y[:, t, :])
                last.then_inc(s_st, 1)
                e.wait_ge(s_st, g + 1)
                e.nop(nofuse=True)
                for t in range(n):
                    last = e.bn_aggr(mv[:, t, :], stats[:, t, :])
                last.then_inc(s_ag, 1)
                e.wait_ge(s_sd, g + 1)
                e.reciprocal(rstd[:, 0:n], sd[:, 0:n]).then_inc(s_rs, 1)
                e.wait_ge(s_rs, g + 1)
                for t in range(n):
                    last = e.tensor_scalar(tile_cols(xs, g, n)[:, t, :], y[:, t, :], mv[:, t, 0:1], rstd[:, t:t + 1],
                                           ALU.subtract, ALU.mult)
                last.then_inc(s_ln, 1)

            e.wait_ge(s_x, 32)
            e.wait_ge(s_w, 16 * W_LOADS)
            sum_tables(0, 0, 0)
            all_groups(e, group)

        @block.tensor
        def _(e):
            e.wait_ge(s_one, 6)
            for w, (n, a, z) in enumerate(TBATCH):
                if a == 0:
                    e.wait_ge(s_pre, 2 + 2 * n)
                if w >= 4:
                    e.wait_ge(s_te, w - 3)
                for j in range(a, z):
                    last = e.transpose(bank[w % 4][:, (j - a) * N_CHUNKS:(j - a + 1) * N_CHUNKS],
                                       rows_f[:, j::COLS], ident[0:N_CHUNKS, 0:N_CHUNKS])
                last.then_inc(s_tp, 1)
            e.wait_ge(s_pre, 10)
            e.matmul(bank[4][:, 0:N_CHUNKS], ones[0:N_CHUNKS, :], diag[:, :], start=True, stop=True)
            e.matmul(bank[5][:, 0:1], ones[0:N_CHUNKS, :], wide[:, :], start=True, stop=True).then_inc(s_b, 1)
            e.wait_ge(s_te, len(TBATCH))
            e.wait_ge(s_pre, PRE_FLAG)

            def spread(d, q, n):
                row = ident_bf[0:N_CHUNKS, bass.ds(d, 1)].to_broadcast([N_CHUNKS, P])
                for k, part in enumerate((rows_hi[n], rows_lo[n])):
                    v = part[:, :].rearrange("c (p q j) -> c q j p", q=QUADS, j=QUAD)
                    last = e.matmul(ps_nodes[q % 2][:, :], row, v[:, q, :, :], start=(k == 0), stop=(k == 1))
                last.then_inc(s_nodes, 1)

            def chunk(i, c, b, d, n, window):
                spread(d, 0, n)
                spread(d, 1, n)
                e.wait_ge(s_lo, c + 1)
                if window:
                    e.wait_ge(s_wev, c + 1)
                for q in range(QUADS):
                    e.wait_ge(s_same, QUADS * c + q + 1)
                    e.wait_ge(s_ev, QUADS * c + q + 1)
                    for j in range(QUAD):
                        t = QUAD * q + j
                        o = j * (D + 1)
                        w = same[q % 2][:, j, :]
                        e.matmul(ps_pay[q % 2][:, o:o + D + 1], w, parts[b][:, t, 0:1 + D], start=True, stop=False)
                        for k in (1, 2):
                            last = e.matmul(ps_pay[q % 2][:, o + 1:o + D + 1], w,
                                            parts[b][:, t, 1 + k * D:1 + (k + 1) * D], start=False, stop=(k == 2))
                    last.then_inc(s_pay, 1)
                    if q + 2 < QUADS:
                        spread(d, q + 2, n)
                    if window:
                        e.wait_ge(s_hot, QUADS * c + q + 1)
                        for j in range(QUAD):
                            t = QUAD * q + j
                            last = e.matmul(ps_win[b][:, 0:3 * D], onehot[q % 2][:, j, :], parts[b][:, t, 1:],
                                            start=(t == 0), stop=(t == COLS - 1))
                        last.then_inc(s_quad, 1)
                    else:
                        e.drain().then_inc(s_quad, 1)

            e.wait_ge(s_rows, 2)
            with e.Fori(0, PAIRS) as i:
                for b in range(2):
                    chunk(i, 2 * i + b, b, 2 * i + b, 0, True)
            again = e.value_load(flag_i[0:1, 0:1], min_val=0, max_val=1)
            with e.If(again > 0):
                with e.Fori(PAIRS, 2 * PAIRS) as i:
                    for b in range(2):
                        chunk(i, 2 * i + b, b, 2 * i + b - N_CHUNKS, 1, False)

            def transposes(g, b):
                e.wait_ge(s_sum, g + 1)
                e.wait_ge(s_xg, g + 1)
                for t in range(tiles_in(g)):
                    e.transpose(bank[b][:, t * P:(t + 1) * P], agg[b][:, t, :], ident)
                    last = e.transpose(bank[2 + b][0:D, t * P:(t + 1) * P], x_now[b][:, t, :], ident)
                last.then_inc(s_nt, 1)

            def group(j, g, b):
                n = tiles_in(g)
                e.wait_ge(s_cat, g + 1)
                for m in range(2):
                    h = bank[4 + m][:, 0:n * P]
                    e.matmul(h, w1io[:, m * P:(m + 1) * P], catT[b][:, 0:n * P], start=True, stop=False)
                    e.matmul(h, w1x[:, m * P:(m + 1) * P], xT[b][:, 0:n * P], start=False, stop=True).then_inc(s_h, 1)
                if not isinstance(g, int) or g < GROUPS:
                    transposes(g + 1, 1 - b)
                e.wait_ge(s_relu, 2 * g + 2)
                e.wait_ge(s_y, g + 1)
                for t in range(n):
                    for m in range(2):
                        last = e.matmul(bank[6 + b][:, t * P:(t + 1) * P], hid[:, m, t * P:(t + 1) * P], w2s[:, m, :],
                                        start=(m == 0), stop=(m == 1))
                last.then_inc(s_o, 1)

            e.wait_ge(s_x, 32)
            e.wait_ge(s_w, 16 * W_LOADS)
            transposes(0, 0)
            all_groups(e, group)


def kernel(x, src, dst, edge_attr_64, L0_gnn_W1, L0_gnn_b1, L0_gnn_W2, L0_gnn_b2):
    import numpy as np
    from concourse import bacc
    from concourse.bass_utils import run_bass_kernel_spmd

    part = np.arange(P, dtype=np.float32)[:, None]
    consts = np.concatenate([np.eye(P, dtype=np.float32), np.tile(part.T, (P, 1)),
                             np.exp2(POW - part), np.exp2(part - POW), part], axis=1).astype(np.float32)
    inputs = {"x": x, "src": src, "dst": dst, "edge_attr": edge_attr_64, "w1": L0_gnn_W1, "b1": L0_gnn_b1,
              "w2": L0_gnn_W2, "b2": L0_gnn_b2, "consts": consts}
    arrays = {f"in_{k}": np.ascontiguousarray(v) for k, v in inputs.items()}
    nc = bacc.Bacc("TRN2", target_bir_lowering=False, num_devices=1)
    args = [nc.dram_tensor(k, v.shape, mybir.dt.from_np(v.dtype), kind="ExternalInput").ap()
            for k, v in arrays.items()]
    out = nc.dram_tensor("out", (N_NODES, D), mybir.dt.float32, kind="ExternalOutput").ap()
    build(nc, *args, out)
    r = run_bass_kernel_spmd(nc, [arrays], core_ids=[0])
    return r.results[0]["out"]
```

```python
from contextlib import ExitStack

import concourse.bass as bass
from concourse import mybir
from concourse.alu_op_type import AluOpType as ALU

N_NODES = 6250
N_EDGES = 200000
D = 64
D_HID = 256
P = 128
EPS = 1e-05

COLS = 16
QUAD = 4
QUADS = COLS // QUAD
CHUNK = P * COLS
N_CHUNKS = -(-N_EDGES // CHUNK)
LAST_EDGES = N_EDGES - (N_CHUNKS - 1) * CHUNK
LAST_PARTS = LAST_EDGES // COLS
PAD = CHUNK - LAST_EDGES
PAIRS = N_CHUNKS // 2
assert N_CHUNKS % 2 == 0 and LAST_EDGES % COLS == 0 and PAD <= LAST_EDGES

OUT_TABLES = 4
TABLE_ROWS = 6400
SPARE = N_NODES
ZERO_TIMES = 5
assert TABLE_ROWS >= N_NODES + P and TABLE_ROWS % P == 0

NT = N_NODES // P
N_TILES = NT + 1
REST = N_NODES - NT * P
GT = 4
assert NT % (2 * GT) == 0

SHARE = 5
SHARE_FROM = COLS - SHARE
SLOTS = P
GROUP_BLOCKS = 7
GROUP_NODES = GROUP_BLOCKS * P
NODE_GROUPS = -(-N_NODES // GROUP_NODES)
UNITS = 4
SHARE_CHUNKS = N_CHUNKS - 2 - NODE_GROUPS * UNITS
SHARE_PAIRS = SHARE_CHUNKS // 2
UNIT_TILES = SHARE_CHUNKS // UNITS
SLOT_W = 3 * D + 2
OH_BUFS = 6
assert SHARE_CHUNKS % 2 == 0 and SHARE_CHUNKS % UNITS == 0
assert NODE_GROUPS * GROUP_NODES <= TABLE_ROWS
ALL_TABLES = OUT_TABLES + 1
CODE = 0x3000
POW = 60


def build(nc, x, src, dst, edges, w1, b1, w2, b2, consts, out):
    fp32 = mybir.dt.float32
    bf16 = mybir.dt.bfloat16
    i32 = mybir.dt.int32
    i16 = mybir.dt.int16
    ACT = mybir.ActivationFunctionType
    AX = mybir.AxisListType

    fp16 = mybir.dt.float16
    out_tab = nc.dram_tensor("out_tables", (ALL_TABLES * TABLE_ROWS, D), fp32, kind="Internal").ap()
    slot_tab = nc.dram_tensor("slot_tiles", (NODE_GROUPS, P, SHARE_CHUNKS * SLOT_W), bf16, kind="Internal").ap()
    in_tab = nc.dram_tensor("in_table", (TABLE_ROWS, D), fp32, kind="Internal").ap()

    with ExitStack() as ctx:
        def sb(name, shape, dt=fp32):
            return ctx.enter_context(nc.sbuf_tensor(name, shape, dt))

        def ps(name, shape):
            return ctx.enter_context(nc.psum_tensor(name, shape, fp32))

        def sem(name):
            return ctx.enter_context(nc.semaphore(name))

        cst = sb("cst", [P, 3 * P + 3 + GROUP_NODES + 2 * NODE_GROUPS + 1])
        ident = cst[:, 0:P]
        iota = cst[:, P:2 * P]
        weight = cst[:, 2 * P:2 * P + 1]
        unweight = cst[:, 2 * P + 1:2 * P + 2]
        part_no = cst[:, 2 * P + 2:2 * P + 3]
        above = cst[:, 2 * P + 3:3 * P + 3]
        iota_group = cst[:, 3 * P + 3:3 * P + 3 + GROUP_NODES]
        group_first = cst[:, 3 * P + 3 + GROUP_NODES:3 * P + 3 + GROUP_NODES + NODE_GROUPS + 1]
        group_slot = cst[:, 3 * P + 4 + GROUP_NODES + NODE_GROUPS:3 * P + 4 + GROUP_NODES + 2 * NODE_GROUPS]
        iota_h = sb("iota_h", [P, GROUP_NODES], fp16)
        above_bf = sb("above_bf", [P, P], bf16)
        nothing = sb("nothing", [P, 6 * D], bf16)
        ones_bf = sb("ones_bf", [P, P], bf16)
        slot = sb("slot", [P, SHARE_CHUNKS + 1, SHARE])
        share_nodes = sb("share_nodes", [P, SHARE_CHUNKS, SHARE, 2], bf16)
        fullest = sb("fullest", [P, 1])
        spare_row = sb("spare_row", [P, 1])
        ident_bf = sb("ident_bf", [P, P], bf16)
        ones = sb("ones", [P, P])
        zeros = sb("zeros", [P, 1, TABLE_ROWS // P // ZERO_TIMES * D])

        rows_i = [None, sb("rows_i1", [N_CHUNKS, CHUNK], i32)]
        rows_code = [sb(f"rows_code{n}", [N_CHUNKS, CHUNK], i16) for n in range(2)]
        cols_code = [sb(f"cols_code{n}", [P, N_CHUNKS, COLS], i16) for n in range(2)]
        cols_f = [sb(f"cols_f{n}", [P, N_CHUNKS, COLS]) for n in range(2)]
        lowest = sb("lowest", [N_CHUNKS, 1])
        highest = sb("highest", [N_CHUNKS, 1])
        wide = sb("wide", [N_CHUNKS, 1])
        diag = sb("diag", [N_CHUNKS, N_CHUNKS])
        base = sb("base", [P, N_CHUNKS])
        off_base = sb("off_base", [P, N_CHUNKS])
        win_at = sb("win_at", [1, 1 + N_CHUNKS], i32)
        shift = sb("shift", [P, 1])
        flag_i = sb("flag_i", [P, 1], i32)

        feat = [sb(f"feat{b}", [P, COLS, D]) for b in range(2)]
        rest = [sb(f"rest{b}", [P, COLS, D]) for b in range(2)]
        parts = [sb(f"parts{b}", [P, COLS, 1 + SLOT_W], bf16) for b in range(2)]
        iota_bf = sb("iota_bf", [P, P], bf16)
        same = [sb(f"same{b}", [P, QUAD, P], bf16) for b in range(2)]
        onehot = [sb(f"onehot{b}", [P, QUAD, P], bf16) for b in range(2)]
        rel = [sb(f"rel{b}", [P, COLS]) for b in range(2)]
        payload = [sb(f"payload{b}", [P, COLS, D]) for b in range(2)]
        weights = [sb(f"weights{b}", [P, COLS]) for b in range(2)]
        win_sum = [sb(f"win_sum{b}", [P, D]) for b in range(2)]
        aggT = sb("aggT", [2 * D, TABLE_ROWS])
        repeated = sb("repeated", [P, COLS])
        target = [sb(f"target{b}", [P, COLS], i32) for b in range(2)]

        with ExitStack() as early:
            def sb_early(name, shape, dt=fp32):
                return early.enter_context(nc.sbuf_tensor(name, shape, dt))

            rows_i[0] = sb_early("rows_i0", [N_CHUNKS, CHUNK], i32)
            rows_f = [sb_early(f"rows_f{n}", [N_CHUNKS, CHUNK]) for n in range(2)]
            from_group = sb_early("from_group", [P, SHARE_CHUNKS, SHARE, NODE_GROUPS + 1], bf16)
            in_group = sb_early("in_group", [P, SHARE_CHUNKS, SHARE, NODE_GROUPS], bf16)
            before = sb_early("before", [P, SHARE_CHUNKS, SHARE + 1, NODE_GROUPS], bf16)
            place = sb_early("place", [P, SHARE_CHUNKS, SHARE, NODE_GROUPS])
            first_slot = sb_early("first_slot", [P, SHARE_CHUNKS, NODE_GROUPS])
            node_i = sb_early("node_i", [P, SHARE_CHUNKS, SHARE], i32)
            node_hi_i = sb_early("node_hi_i", [P, SHARE_CHUNKS, SHARE], i32)
        with ExitStack() as middle:
            def sb_middle(name, shape, dt=fp32):
                return middle.enter_context(nc.sbuf_tensor(name, shape, dt))

            to_slot = [sb_middle(f"to_slot{b}", [P, SHARE, GROUP_NODES], bf16) for b in range(2)]
            slots_out = [sb_middle(f"slots_out{b}", [P, NODE_GROUPS, SLOT_W], bf16) for b in range(2)]
            slots_in = [sb_middle(f"slots_in{b}", [P, UNIT_TILES, SLOT_W], bf16) for b in range(2)]
            to_node = [sb_middle(f"to_node{k}", [P, GROUP_NODES], bf16) for k in range(OH_BUFS)]
            slot_rel = [sb_middle(f"slot_rel{b}", [P, UNIT_TILES]) for b in range(2)]
            group_sum = sb_middle("group_sum", [P, GROUP_BLOCKS, D])
        with ExitStack() as late:
            def sb_late(name, shape, dt=fp32):
                return late.enter_context(nc.sbuf_tensor(name, shape, dt))

            tabs = [sb_late(f"tabs{b}", [P, ALL_TABLES, GT * D]) for b in range(2)]
            xT = [sb_late(f"xT{b}", [D, GT * P]) for b in range(2)]
            y = sb_late("y", [P, GT, D])
            y_sum = sb_late("y_sum", [P, GT, D])
            hid = [sb_late(f"hid{b}", [P, 2, GT * P]) for b in range(2)]
        share_edges = SHARE_CHUNKS * SHARE
        sb("room", [P, 3 * CHUNK + share_edges * (NODE_GROUPS + 1) // 2 + share_edges * NODE_GROUPS // 2
                    + SHARE_CHUNKS * (SHARE + 1) * NODE_GROUPS // 2 + share_edges * NODE_GROUPS
                    + SHARE_CHUNKS * NODE_GROUPS + 2 * share_edges + 2 * P])

        w1io = sb("w1io", [P, D_HID])
        w1x = sb("w1x", [D, D_HID])
        w2s = sb("w2s", [P, 2, 2 * D])
        b1s = sb("b1s", [P, 2])
        b2s = sb("b2s", [P, D])
        xs = sb("xs", [P, N_TILES, D])

        bank = [ps(f"bank{n}", [P, 512]) for n in range(8)]
        ps_nodes = bank[0]
        ps_pay = bank[1]
        ps_win = bank[2]
        ps_winT = bank[3][0:D, 0:P]
        ps_share = bank[4:8]

        s_cst = sem("s_cst")
        s_row = [sem(f"s_row{n}") for n in range(2)]
        s_w = sem("s_w")
        s_x = sem("s_x")
        s_xz = sem("s_xz")
        s_one = sem("s_one")
        s_zero = sem("s_zero")
        s_pad = sem("s_pad")
        s_pre = sem("s_pre")
        s_tp = sem("s_tp")
        s_te = sem("s_te")
        s_b = sem("s_b")
        s_f = [sem(f"s_f{n}") for n in range(2)]
        s_codes = sem("s_codes")
        s_feat = [sem(f"s_feat{b}") for b in range(2)]
        s_hi = sem("s_hi")
        s_rest = sem("s_rest")
        s_mid = sem("s_mid")
        s_lo = sem("s_lo")
        s_nodes = sem("s_nodes")
        s_same = sem("s_same")
        s_hot = sem("s_hot")
        s_rel = sem("s_rel")
        s_pay = sem("s_pay")
        s_quad = sem("s_quad")
        s_ev = sem("s_ev")
        s_wsum = sem("s_wsum")
        s_wT = sem("s_wT")
        s_wadd = sem("s_wadd")
        s_rep = sem("s_rep")
        s_tgt = sem("s_tgt")
        s_free = sem("s_free")
        s_tab = [sem(f"s_tab{k}") for k in range(OUT_TABLES)]
        s_in = sem("s_in")
        s_inl = sem("s_inl")
        s_in_ready = sem("s_in_ready")
        s_inT = sem("s_inT")
        s_ranks = sem("s_ranks")
        s_nodes_in = sem("s_nodes_in")
        s_to_slot = sem("s_to_slot")
        s_slot = sem("s_slot")
        s_slot_ev = sem("s_slot_ev")
        s_slot_out = [sem(f"s_slot_out{b}") for b in range(2)]
        s_slot_in = [sem(f"s_slot_in{b}") for b in range(2)]
        s_slot_rel = sem("s_slot_rel")
        s_to_node = sem("s_to_node")
        s_tile = sem("s_tile")
        s_sums = sem("s_sums")
        s_flush = sem("s_flush")
        s_share_out = sem("s_share_out")
        s_tail = sem("s_tail")
        s_ina = sem("s_ina")
        s_agg = sem("s_agg")

        GROUPS = NT // GT
        x_out = [sb(f"x_out{b}", [P, GT, 2 * D]) for b in range(2)]
        stats = sb("stats", [P, GT, 6])
        mv = sb("mv", [P, GT, 2])
        var_eps = sb("var_eps", [P, GT])
        minus_half = sb("minus_half", [P, GT])
        in_now = sb("in_now", [P, D])
        rstd = sb("rstd", [P, GT])
        s_load = [sem(f"s_load{b}") for b in range(2)]
        s_sum = sem("s_sum")
        s_xg = sem("s_xg")
        s_nt = sem("s_nt")
        s_cat = sem("s_cat")
        s_h = sem("s_h")
        s_relu = sem("s_relu")
        s_o = sem("s_o")
        s_y = sem("s_y")
        s_yb = sem("s_yb")
        s_st = sem("s_st")
        s_ag = sem("s_ag")
        s_mv = sem("s_mv")
        s_rs = sem("s_rs")
        s_ln = sem("s_ln")
        s_out = sem("s_out")
        PRE_FLAG = 25
        W_LOADS = 5
        block = ctx.enter_context(nc.Block())

        class Mode:
            def __init__(self, n, cols=COLS, window=False, share=False, sums=False, only=0):
                self.n, self.cols, self.window, self.share, self.sums, self.only = n, cols, window, share, sums, only
                self.quads = [(QUAD * q, min(QUAD, cols - QUAD * q)) for q in range(-(-cols // QUAD))]

        SHARING = Mode(0, SHARE_FROM, window=True, share=True)
        SUMMING = Mode(0, window=True, sums=True)
        PLAIN = Mode(0, window=True)
        BY_DST = Mode(1)
        SHARE_BY_SRC = Mode(0, only=SHARE_FROM)
        SHARE_QUADS = len(SHARING.quads)
        assert SHARE_QUADS % 2 == 1

        def quad_no(c, mode):
            return SHARE_QUADS * c if mode is SHARING else QUADS * c - (QUADS - SHARE_QUADS) * SHARE_CHUNKS

        def quad_buf(q, b, mode):
            return (b + q) % 2 if mode is SHARING else q % 2

        def main_loop(e, pair, before_group=None, after_group=None):
            with e.Fori(0, SHARE_PAIRS) as i:
                pair(i, SHARING, None)
            with e.Fori(0, NODE_GROUPS) as g:
                if before_group:
                    before_group(g)
                with e.Fori(0, UNITS // 2) as k:
                    pair(g * (UNITS // 2) + k + SHARE_PAIRS, SUMMING, (g, k))
                if after_group:
                    after_group(g)
            pair(PAIRS - 1, PLAIN, None)

        row_view = [v[0:(N_CHUNKS - 1) * CHUNK].rearrange("(c k) -> c k", k=CHUNK) for v in (src, dst)]
        ROUNDS = -(-NODE_GROUPS // 2)
        SLOT_PARTS = [(0, 6), (6, 12), (12, UNIT_TILES)]
        PRE_RANKS = 20

        def unit_tiles(q):
            return range(UNIT_TILES * q // QUADS, UNIT_TILES * (q + 1) // QUADS)

        TB = 5
        TBATCH = [(n, a, min(a + TB, COLS)) for n in range(2) for a in range(0, COLS, TB)]
        BATCHES = len(TBATCH) // 2

        def tiles_of(t, g, lead=0):
            if isinstance(g, int) and g == GROUPS:
                return t[lead + NT * P:lead + (NT + 1) * P, :]
            return t[bass.ds(g * (GT * P) + lead, GT * P), :].rearrange("(p t) d -> p (t d)", t=GT)

        def tiles_in(g):
            return 1 if isinstance(g, int) and g == GROUPS else GT

        def tile_cols(t, g, n):
            return t[:, bass.ds(g * GT, n), :]

        def all_groups(e, group):
            with e.Fori(0, GROUPS // 2 - 2) as j:
                for b in range(2):
                    group(j, 2 * j + b, b)
            for g in range(GROUPS - 4, GROUPS + 1):
                group(g // 2, g, g % 2)

        @block.sync
        def _(e):
            for n, v in enumerate((src, dst)):
                full = (N_CHUNKS - 1) // 16 * 16
                e.dma_start(rows_i[n][0:full, :], row_view[n][0:full, :]).then_inc(s_row[n], 16)
                e.dma_start(rows_i[n][full:N_CHUNKS - 1, :], row_view[n][full:, :]).then_inc(s_row[n], 16)
                last = v[(N_CHUNKS - 1) * CHUNK:N_EDGES].rearrange("(a k) -> a k", a=1)
                e.dma_start(rows_i[n][N_CHUNKS - 1:N_CHUNKS, 0:LAST_EDGES], last).then_inc(s_row[n], 16)
                e.dma_start(rows_i[n][N_CHUNKS - 1:N_CHUNKS, LAST_EDGES:CHUNK],
                            last[:, LAST_EDGES - PAD:LAST_EDGES]).then_inc(s_row[n], 16)

            def load_chunks(pair, first_chunk, last_pair):
                for b in range(2):
                    c = first_chunk + b
                    e.wait_ge(s_rest, c + 1)
                    if last_pair and b == 1:
                        e.wait_ge(s_pad, 1 if first_chunk == N_CHUNKS - 2 else 2)
                        at, parts_of = (N_CHUNKS - 1) * CHUNK, ((0, P // 2), (P // 2, LAST_PARTS))
                    else:
                        at, parts_of = (2 * pair + b) * CHUNK, ((0, P // 2), (P // 2, P))
                    for lo, hi in parts_of:
                        e.dma_start(feat[b][lo:hi, :, :],
                                    edges[bass.ds(at + lo * COLS, (hi - lo) * COLS), :].rearrange(
                                        "(p j) d -> p j d", j=COLS)).then_inc(s_feat[b], 16)

            def load_pair(i, mode, at):
                if mode is not SUMMING:
                    load_chunks(i, 2 * i, mode is PLAIN)
                    return
                g, k = at
                load_chunks(i, 2 * i, False)
                for b in range(2):
                    e.wait_ge(s_slot_out[b], 32 * (SHARE_PAIRS + 1))
                for b in range(2):
                    u = UNITS * g + 2 * k + b
                    e.wait_ge(s_tile, UNIT_TILES * (u + 1) + 1)
                    for lo, hi in SLOT_PARTS:
                        e.dma_start(slots_in[b][:, lo:hi, :].rearrange("p t w -> p (t w)"),
                                    slot_tab[bass.ds(g, 1), :, bass.ds(((2 * k + b) * UNIT_TILES + lo) * SLOT_W,
                                                                       (hi - lo) * SLOT_W)
                                             ].rearrange("g p w -> p (g w)")).then_inc(s_slot_in[b], 16)

            with e.Fori(0, SHARE_PAIRS) as i:
                load_pair(i, SHARING, None)
            with e.Fori(0, NODE_GROUPS) as g:
                with e.Fori(0, UNITS // 2) as k:
                    load_pair(g * (UNITS // 2) + k + SHARE_PAIRS, SUMMING, (g, k))
            load_pair(PAIRS - 1, PLAIN, None)

            e.wait_ge(s_pre, PRE_FLAG)
            again = e.value_load(flag_i[0:1, 0:1], min_val=0, max_val=1)
            with e.If(again > 0):
                with e.Fori(PAIRS, 2 * PAIRS - 1) as i:
                    load_chunks(i - PAIRS, 2 * i, False)
                load_chunks(PAIRS - 1, 2 * (2 * PAIRS - 1), True)
                with e.Fori(2 * PAIRS, 2 * PAIRS + SHARE_PAIRS) as i:
                    load_chunks(i - 2 * PAIRS, 2 * i, False)
                with e.Fori(0, N_TILES) as i:
                    e.wait_ge(s_ina, i + 1)
                    e.dma_start(in_now[:, :], in_tab[bass.ds(i * P, P), :]).then_inc(s_inl, 16)

            def load_group(g, b):
                n = tiles_in(g)
                for k in range(ALL_TABLES):
                    e.dma_start(tabs[b][:, k, 0:n * D], tiles_of(out_tab, g, k * TABLE_ROWS)).then_inc(s_load[b], 16)

            def group(j, g, b):
                if not isinstance(g, int) or g + 2 <= GROUPS:
                    e.wait_ge(s_sum, g + 1)
                    load_group(g + 2, b)

            e.wait_ge(s_agg, 1)
            e.wait_ge(s_share_out, 16 * (NODE_GROUPS + 1))
            e.wait_ge(s_tail, 3)
            load_group(0, 0)
            load_group(1, 1)
            all_groups(e, group)

        @block.gpsimd
        def _(e):
            e.sem_inc(s_free, 3)
            e.wait_ge(s_zero, 1)
            for n in range(2):
                e.wait_ge(s_row[n], 64)

            def clear(table, s):
                e.dma_start(table.rearrange("(p t r) d -> p t (r d)", p=P, t=ZERO_TIMES),
                            zeros[:, :, :].to_broadcast([P, ZERO_TIMES, zeros.shape[2]])).then_inc(s, 16)

            for k in range(OUT_TABLES):
                clear(out_tab[k * TABLE_ROWS:(k + 1) * TABLE_ROWS, :], s_tab[k])
            e.memset(aggT[:, :], 0.0).then_inc(s_wadd, 1)

            def uses(k, cols):
                return len(range(k, cols, OUT_TABLES))

            def add_chunk(c, b, mode):
                e.wait_ge(s_tgt, c + 1)
                for t in range(mode.cols):
                    if t % QUAD == 0:
                        e.wait_ge(s_ev, quad_no(c, mode) + t // QUAD + 3)
                    at = bass.IndirectOffsetOnAxis(ap=target[b][:, t:t + 1], axis=0)
                    if mode.window:
                        k, turn = t % OUT_TABLES, t // OUT_TABLES + 1
                        if mode is SHARING:
                            before_it = uses(k, SHARE_FROM) * c + turn
                        else:
                            before_it = uses(k, COLS) * c + (
                                turn - (uses(k, COLS) - uses(k, SHARE_FROM)) * SHARE_CHUNKS)
                        e.wait_ge(s_tab[k], 16 * before_it)
                        e.nop(nofuse=True)
                        e.indirect_dma_start(out_tab, at, payload[b][:, t, :], None,
                                             element_offset=k * TABLE_ROWS * D, compute_op=ALU.add).then_inc(s_tab[k], 16)
                    else:
                        e.wait_ge(s_in, 16 * (COLS * (c - N_CHUNKS) + t + 1))
                        e.nop(nofuse=True)
                        e.indirect_dma_start(in_tab if mode is BY_DST else out_tab, at, payload[b][:, t, :], None,
                                             compute_op=ALU.add).then_inc(s_in, 16)
                    if t in (QUAD - 1, 2 * QUAD - 1):
                        e.sem_inc(s_free, 1)

            def add_pair(i, mode, at):
                for b in range(2):
                    add_chunk(2 * i + b, b, mode)

            main_loop(e, add_pair)
            for k in range(OUT_TABLES):
                e.wait_ge(s_tab[k], 16 * (uses(k, COLS) * (N_CHUNKS - SHARE_CHUNKS) + uses(k, SHARE_FROM) * SHARE_CHUNKS + 1))
            e.wait_ge(s_pre, PRE_FLAG)
            again = e.value_load(flag_i[0:1, 0:1], min_val=0, max_val=1)
            with e.If(again > 0):
                clear(in_tab, s_in)
                with e.Fori(PAIRS, 2 * PAIRS) as i:
                    add_pair(i, BY_DST, None)
                with e.Fori(2 * PAIRS, 2 * PAIRS + SHARE_PAIRS) as i:
                    add_pair(i, SHARE_BY_SRC, None)
                e.wait_ge(s_in, 16 * (COLS * (N_CHUNKS + SHARE_CHUNKS) + 1))
                e.sem_inc(s_ina, 1)
            e.sem_inc(s_agg, 1)

            def group(j, g, b):
                e.wait_ge(s_ag, g + 1)
                e.nop(nofuse=True)
                e.tensor_tensor(rstd[:, 0:tiles_in(g)], var_eps[:, 0:tiles_in(g)], minus_half[:, 0:tiles_in(g)],
                                ALU.pow).then_inc(s_rs, 1)
                e.wait_ge(s_ln, g + 1)
                if isinstance(g, int) and g == GROUPS:
                    e.dma_start(out[NT * P:N_NODES, :], xs[0:REST, NT, :]).then_inc(s_out, 16)
                else:
                    e.dma_start(tiles_of(out, g), tile_cols(xs, g, GT).rearrange("p r d -> p (r d)")).then_inc(s_out, 16)

            all_groups(e, group)
            e.wait_ge(s_out, 16 * (GROUPS + 1))

        @block.scalar
        def _(e):
            e.dma_start(cst[:, :], consts).then_inc(s_cst, 16)
            e.wait_ge(s_pre, 1)
            e.sem_inc(s_ev, 2)
            for n in range(2):
                e.wait_ge(s_row[n], 64)
                e.activation(rows_f[n][:, :], rows_i[n][:, :], ACT.Copy).then_inc(s_f[n], 1)
            for w, (n, a, z) in enumerate(TBATCH):
                e.wait_ge(s_tp, w + 1)
                e.activation(cols_f[n][:, :, a:z].rearrange("p c j -> p j c"),
                             bank[w % 4][:, 0:(z - a) * N_CHUNKS].rearrange("p (j c) -> p j c", c=N_CHUNKS),
                             ACT.Copy).then_inc(s_te, 1)
            e.dma_start(w1io[:, :], w1[0:2 * D, :]).then_inc(s_w, 16)
            e.dma_start(w1x[:, :], w1[2 * D:3 * D, :]).then_inc(s_w, 16)
            e.dma_start(w2s[:, :, 0:D], w2.rearrange("(a p) n -> p a n", p=P)).then_inc(s_w, 16)
            with nc.allow_non_contiguous_dma(reason="256 biases, once"):
                e.dma_start(b1s[:, :], b1.rearrange("(a p) -> p a", p=P)).then_inc(s_w, 16)
            e.dma_start(b2s[:, :], b2.rearrange("(a n) -> a n", a=1).to_broadcast([P, D])).then_inc(s_w, 16)
            e.wait_ge(s_xz, 1)
            e.dma_start(xs[:, 0:NT, :].rearrange("p (g t) d -> p g (t d)", t=GT),
                        x[0:NT * P, :].rearrange("(g p t) d -> p g (t d)", p=P, t=GT)).then_inc(s_x, 16)
            e.dma_start(xs[0:REST, NT, :], x[NT * P:, :]).then_inc(s_x, 16)

            def split_hi(i, c, b):
                e.wait_ge(s_feat[b], 32 * (i + 1))
                e.wait_ge(s_quad, QUADS * c + 1)
                e.activation(parts[b][:, :, 1:1 + D], feat[b][:, :, :], ACT.Copy).then_inc(s_hi, 1)

            def split_mid(c, b):
                e.wait_ge(s_rest, c + 3)
                e.activation(parts[b][:, :, 1 + D:1 + 2 * D], rest[b][:, :, :], ACT.Copy).then_inc(s_mid, 1)

            def slots(i, c, b, mode, rounds):
                for r in rounds if mode.share else []:
                    if r == 0:
                        e.wait_ge(s_slot_out[b], 32 * (i + 1))
                    e.wait_ge(s_slot, ROUNDS * c + r + 1)
                    n = min(2, NODE_GROUPS - 2 * r)
                    e.activation(slots_out[b][:, 2 * r:2 * r + n, :],
                                 ps_share[r % 2][:, 0:n * SLOT_W].rearrange("p (g w) -> p g w", w=SLOT_W),
                                 ACT.Copy).then_inc(s_slot_ev, 1)

            def chunk(i, c, b, mode, ahead):
                if ahead:
                    split_hi(i + b, c + 1, 1 - b)
                if mode.share:
                    e.activation(parts[b][:, SHARE_FROM:COLS, 1 + 3 * D:1 + SLOT_W],
                                 share_nodes[:, bass.ds(c, 1), :, :].rearrange("p a k w -> p (a k) w"),
                                 ACT.Copy).then_inc(s_nodes_in, 1)
                for q, (t, n) in enumerate(mode.quads):
                    if q < 2:
                        e.wait_ge(s_free, 2 * c + 1 + q)
                    e.wait_ge(s_pay, quad_no(c, mode) + q + 1)
                    quad = ps_pay[:, 0:n * (D + 1)].rearrange("p (t d) -> p t d", d=D + 1)
                    e.activation(payload[b][:, t:t + n, :], quad[:, :, 1:D + 1], ACT.Copy)
                    e.activation(weights[b][:, t:t + n], quad[:, :, 0], ACT.Copy).then_inc(s_ev, 1)
                    if ahead and q == 0:
                        split_mid(c + 1, 1 - b)
                    slots(i, c, b, mode, [q])
                slots(i, c, b, mode, range(len(mode.quads), ROUNDS))
                if mode.share:
                    for lo, hi in ((0, NODE_GROUPS // 2 + 1), (NODE_GROUPS // 2 + 1, NODE_GROUPS)):
                        e.wait_ge(s_slot_ev, ROUNDS * c + -(-hi // 2) + 2)
                        e.dma_start(slot_tab[lo:hi, :, bass.ds(c * SLOT_W, SLOT_W)].rearrange("g p w -> p g w"),
                                    slots_out[b][:, lo:hi, :]).then_inc(s_slot_out[b], 16)

            def chunk_pair(i, mode, at):
                for b in range(2):
                    chunk(i, 2 * i + b, b, mode, mode is not PLAIN or b == 0)

            def store_group(g):
                e.wait_ge(s_flush, g + 2)
                e.dma_start(out_tab[bass.ds(g * GROUP_NODES + OUT_TABLES * TABLE_ROWS, GROUP_NODES), :].rearrange(
                    "(a p) d -> p a d", p=P), group_sum[:, :, :]).then_inc(s_share_out, 16)

            def prologue(pair):
                split_hi(pair, 2 * pair, 0)
                split_mid(2 * pair, 0)

            prologue(0)
            main_loop(e, chunk_pair, after_group=store_group)
            e.wait_ge(s_pre, PRE_FLAG)
            again = e.value_load(flag_i[0:1, 0:1], min_val=0, max_val=1)
            with e.If(again > 0):
                prologue(PAIRS)
                with e.Fori(PAIRS, 2 * PAIRS - 1) as i:
                    chunk_pair(i, BY_DST, None)
                for b in range(2):
                    chunk(2 * PAIRS - 1, 4 * PAIRS - 2 + b, b, BY_DST, b == 0)
                prologue(2 * PAIRS)
                with e.Fori(2 * PAIRS, 2 * PAIRS + SHARE_PAIRS - 1) as i:
                    chunk_pair(i, SHARE_BY_SRC, None)
                for b in range(2):
                    chunk(2 * PAIRS + SHARE_PAIRS - 1, 2 * (2 * PAIRS + SHARE_PAIRS - 1) + b, b, SHARE_BY_SRC, b == 0)
            e.sem_inc(s_tail, 1)

            def out_of_transposes(g, b):
                n = tiles_in(g) * P
                e.wait_ge(s_nt, g + 1)
                e.activation(aggT[D:2 * D, bass.ds(g * (GT * P), n)], bank[b][D:2 * D, 0:n], ACT.Copy)
                e.activation(xT[b][:, 0:n], bank[b][0:D, 0:n], ACT.Copy).then_inc(s_cat, 1)

            def group(j, g, b):
                n = tiles_in(g) * P
                e.wait_ge(s_o, g + 1)
                for m in range(2):
                    e.wait_ge(s_h, 2 * g + m + 1)
                    e.activation(hid[b][:, m, 0:n], bank[4 + m][:, 0:n], ACT.Relu,
                                 bias=b1s[:, m:m + 1]).then_inc(s_relu, 1)
                if not isinstance(g, int) or g < GROUPS:
                    out_of_transposes(g + 1, 1 - b)

            e.wait_ge(s_w, 16 * W_LOADS)
            out_of_transposes(0, 0)
            all_groups(e, group)

        @block.vector
        def _(e):
            steps = [0]

            def step(ins):
                steps[0] += 1
                ins.then_inc(s_pre, 1)
                e.wait_ge(s_pre, steps[0])

            e.memset(zeros[:, :, :], 0.0).then_inc(s_zero, 1)
            e.memset(ones[:, :], 1.0).then_inc(s_one, 1)
            e.memset(xs[96:P, NT, :], 0.0).then_inc(s_xz, 1)
            e.memset(minus_half[:, :], -0.5)
            e.memset(w2s[:, :, D:2 * D], 0.0)
            step(e.memset(win_at[:, :], 0))
            for s, first in ((s_wsum, 1), (s_wadd, 1), (s_rest, 2), (s_y, 2), (s_o, 2), (s_quad, QUADS + 1),
                             (s_tile, 2 * UNIT_TILES + 1), (s_slot_ev, 2), (s_flush, 1), (s_share_out, 16),
                             (s_slot_out[0], 32), (s_slot_out[1], 32)):
                e.sem_inc(s, first)

            e.wait_ge(s_row[0], 64)
            step(e.tensor_scalar(rows_code[0][:, :], rows_i[0][:, :], CODE, None, ALU.add))
            e.wait_ge(s_cst, 16)
            e.tensor_copy(ident_bf[:, :], ident).then_inc(s_one, 1)
            e.tensor_copy(iota_bf[:, :], iota)
            e.tensor_copy(iota_h[:, :], iota_group)
            e.tensor_copy(above_bf[:, :], above)
            e.memset(ones_bf[:, :], 1.0)
            e.memset(slot[:, SHARE_CHUNKS, :], -1.0)
            e.memset(nothing[:, :], 0.0)
            e.memset(before[:, :, 0, :], 0.0).then_inc(s_one, 1)
            for b in range(2):
                e.tensor_copy(parts[b][:, :, 0], weight.to_broadcast([P, COLS])).then_inc(s_one, 1)
            e.tensor_scalar(spare_row[:, :], part_no, float(SPARE), None, ALU.add).then_inc(s_one, 1)
            e.wait_ge(s_row[1], 64)
            step(e.tensor_reduce(lowest[:, :], rows_i[1][:, :], AX.X, ALU.min))
            step(e.tensor_reduce(highest[:, :], rows_i[1][:, :], AX.X, ALU.max))
            step(e.tensor_tensor(wide[:, :], highest[:, :], lowest[:, :], ALU.subtract))
            step(e.tensor_scalar(wide[:, :], wide[:, :], P - 0.5, None, ALU.is_gt))
            step(e.tensor_scalar(diag[:, :], ident[0:N_CHUNKS, 0:N_CHUNKS], lowest[:, 0:1], None, ALU.mult))
            e.wait_ge(s_b, 1)
            step(e.tensor_copy(base[:, :], bank[4][:, 0:N_CHUNKS]))
            step(e.tensor_copy(win_at[:, 1:], bank[4][0:1, 0:N_CHUNKS]))
            step(e.tensor_scalar(shift[:, :], bank[5][:, 0:1], 0.5, None, ALU.is_gt))
            e.wait_ge(s_te, BATCHES)
            e.wait_ge(s_one, 6)
            step(e.tensor_scalar(cols_code[0][:, :, :], cols_f[0][:, :, :], float(CODE), None, ALU.add))
            share = cols_f[0][:, 0:SHARE_CHUNKS, SHARE_FROM:COLS]
            whole = [P, SHARE_CHUNKS * SHARE]
            step(e.tensor_copy(node_i[:, :, :], share))
            step(e.tensor_scalar(node_hi_i[:, :, :], node_i[:, :, :], 0x1F80, None, ALU.bitwise_and))
            e.tensor_copy(share_nodes[:, :, :, 0], node_hi_i[:, :, :])
            e.tensor_tensor(share_nodes[:, :, :, 1], node_i[:, :, :], node_hi_i[:, :, :], ALU.subtract)
            for k in range(SHARE):
                last = e.tensor_tensor(
                    from_group[:, :, k, :],
                    cols_f[0][:, 0:SHARE_CHUNKS, SHARE_FROM + k:SHARE_FROM + k + 1].to_broadcast(
                        [P, SHARE_CHUNKS, NODE_GROUPS + 1]),
                    group_first.rearrange("p (a g) -> p a g", a=1).to_broadcast([P, SHARE_CHUNKS, NODE_GROUPS + 1]),
                    ALU.is_ge)
            step(last)
            step(e.tensor_tensor(in_group[:, :, :, :].rearrange("p c k g -> p (c k) g"),
                                 from_group[:, :, :, 0:NODE_GROUPS].rearrange("p c k g -> p (c k) g"),
                                 from_group[:, :, :, 1:].rearrange("p c k g -> p (c k) g"), ALU.subtract))
            for k in range(SHARE):
                step(e.tensor_tensor(before[:, :, k + 1, :], before[:, :, k, :], in_group[:, :, k, :], ALU.add))
            e.wait_ge(s_ranks, 1)
            ranks = bank[6][:, 0:SHARE_CHUNKS * NODE_GROUPS].rearrange("p (c g) -> p c g", g=NODE_GROUPS)
            step(e.tensor_tensor(first_slot[:, :, :], ranks, group_slot.rearrange("p (a g) -> p a g", a=1).to_broadcast(
                [P, SHARE_CHUNKS, NODE_GROUPS]), ALU.add))
            step(e.tensor_reduce(fullest[:, :], bank[7][:, 0:SHARE_CHUNKS * NODE_GROUPS], AX.X, ALU.max))
            step(e.tensor_scalar(fullest[:, :], fullest[:, :], SLOTS + 0.5, None, ALU.is_gt))
            step(e.tensor_tensor(shift[:, :], shift[:, :], fullest[:, :], ALU.max))
            step(e.tensor_copy(flag_i[:, :], shift[:, :]))
            assert steps[0] == PRE_FLAG, steps
            step(e.tensor_scalar(shift[:, :], shift[:, :], float(1 << 14), None, ALU.mult))
            for k in range(SHARE):
                last = e.tensor_tensor(place[:, :, k, :], before[:, :, k, :], first_slot[:, :, :], ALU.add)
            step(last)
            step(e.tensor_tensor(place[:, :, :, :].rearrange("p c k g -> p (c k g)"),
                                 place[:, :, :, :].rearrange("p c k g -> p (c k g)"),
                                 in_group[:, :, :, :].rearrange("p c k g -> p (c k g)"), ALU.mult))
            step(e.tensor_reduce(slot[:, 0:SHARE_CHUNKS, :].rearrange("p c k -> p (c k)"),
                                 place[:, :, :, :].rearrange("p c k g -> p (c k) g"), AX.X, ALU.add))
            step(e.tensor_scalar(slot[:, :, :], slot[:, :, :], shift[:, 0:1], None, ALU.subtract))
            step(e.tensor_scalar(off_base[:, :], base[:, :], shift[:, 0:1], None, ALU.subtract))
            e.wait_ge(s_te, 2 * BATCHES)
            e.wait_ge(s_one, 6)

            def split_rest(c, b):
                e.wait_ge(s_hi, c + 1)
                e.tensor_tensor(rest[b][:, :, :], feat[b][:, :, :], parts[b][:, :, 1:1 + D],
                                ALU.subtract).then_inc(s_rest, 1)

            def split_lo(c, b):
                e.wait_ge(s_mid, c + 1)
                e.tensor_tensor(parts[b][:, :, 1 + 2 * D:1 + 3 * D], rest[b][:, :, :],
                                parts[b][:, :, 1 + D:1 + 2 * D], ALU.subtract).then_inc(s_lo, 1)

            def add_window(c, b, d):
                at = e.value_load(win_at[0:1, bass.ds(d, 1)], min_val=0, max_val=N_NODES)
                e.wait_ge(s_wT, c + 1)
                e.wait_ge(s_wadd, c + 2)
                e.tensor_tensor(aggT[0:D, bass.ds(at, P)], aggT[0:D, bass.ds(at, P)], ps_winT,
                                ALU.add).then_inc(s_wadd, 1)

            def to_slots(c, b, columns):
                for k in columns:
                    last = e.tensor_scalar(to_slot[b][:, k, :], iota_h[:, :],
                                           slot[:, bass.ds(c, 1), k:k + 1].rearrange("p a k -> p (a k)"),
                                           None, ALU.is_equal)
                if SHARE - 1 in columns:
                    last.then_inc(s_to_slot, 1)

            def tiles_to_nodes(u, b, tiles):
                for i in tiles:
                    last_user = i - OH_BUFS
                    if last_user < 0:
                        last_user = max(range(i, UNIT_TILES, OH_BUFS)) - UNIT_TILES
                    e.wait_ge(s_tile, UNIT_TILES * u + last_user + 2 + 2 * UNIT_TILES)
                    e.nop(nofuse=True)
                    e.tensor_scalar(to_node[i % OH_BUFS][:, :], iota_h[:, :], slot_rel[b][:, i:i + 1], None,
                                    ALU.is_equal).then_inc(s_to_node, 1)

            def read_window(c, b):
                e.wait_ge(s_quad, QUADS * c + 5)
                e.tensor_reduce(win_sum[1 - b][:, :], ps_win[:, 0:3 * D].rearrange("p (k d) -> p d k", k=3),
                                AX.X, ALU.add).then_inc(s_wsum, 1)

            def chunk(c, b, d, mode, ahead, group, u):
                if mode.window:
                    e.wait_ge(s_quad, QUADS * c + 1)
                    e.tensor_scalar(rel[b][:, :], cols_f[1][:, bass.ds(d, 1), :].rearrange("p a j -> p (a j)"),
                                    off_base[:, bass.ds(d, 1)], None, ALU.subtract).then_inc(s_rel, 1)
                for q in range(QUADS):
                    e.wait_ge(s_quad, QUADS * c + q + 4)
                    if q < len(mode.quads):
                        t, n = mode.quads[q]
                        e.wait_ge(s_nodes, quad_no(c, mode) + q + 1)
                        own = cols_code[mode.n][:, bass.ds(d, 1), t:t + n].bitcast(bf16).rearrange(
                            "p a (j k) -> p (a j) k", k=1).to_broadcast([P, n, P])
                        e.tensor_tensor(same[quad_buf(q, b, mode)][:, 0:n, :],
                                        ps_nodes[:, 0:n * P].rearrange("p (j k) -> p j k", k=P),
                                        own, ALU.is_equal).then_inc(s_same, 1)
                    if mode.window:
                        if q == 0:
                            e.wait_ge(s_rel, c + 1)
                        for j in range(QUAD):
                            hot = e.tensor_scalar(onehot[q % 2][:, j, :], iota_bf[:, :],
                                                  rel[b][:, QUAD * q + j:QUAD * q + j + 1], None, ALU.is_equal)
                        hot.then_inc(s_hot, 1)
                        if q == 0:
                            read_window(c, b)
                    if mode.share and q > 0:
                        to_slots(c + 1, 1 - b, range(2 * q - 2, min(2 * q, SHARE)))
                    if mode.sums:
                        if q == 0:
                            e.wait_ge(s_slot_in[b], group[1])
                            e.nop(nofuse=True)
                            e.scalar_tensor_tensor(slot_rel[b][:, :], slots_in[b][:, :, 3 * D],
                                                   group_first[:, bass.ds(group[0], 1)], slots_in[b][:, :, 3 * D + 1],
                                                   ALU.subtract, ALU.add).then_inc(s_slot_rel, 1)
                            e.wait_ge(s_slot_rel, u + 1)
                        tiles_to_nodes(u, b, unit_tiles(q))
                    if ahead and q == 0:
                        split_rest(c + 1, 1 - b)
                    if mode.window and q == 1:
                        add_window(c, b, d)
                    if ahead and q == 2:
                        split_lo(c + 1, 1 - b)
                e.wait_ge(s_ev, quad_no(c, mode) + len(mode.quads) + 2)
                e.wait_ge(s_free, 2 * c + 2)
                n = mode.cols
                e.tensor_scalar(repeated[:, 0:n], weights[b][:, 0:n], unweight, 2.5, ALU.mult, ALU.is_ge).then_inc(s_rep, 1)
                e.wait_ge(s_rep, c + 1)
                first = mode.only
                ins = e.scalar_tensor_tensor(target[b][:, first:n], repeated[:, first:n], spare_row[:, 0:1],
                                             cols_f[mode.n][:, bass.ds(d, 1), first:n].rearrange("p a j -> p (a j)"),
                                             ALU.mult, ALU.max)
                if first:
                    ins = e.tensor_copy(target[b][:, 0:first], spare_row[:, 0:1].to_broadcast([P, first]))
                ins.then_inc(s_tgt, 1)

            def pad(c):
                e.wait_ge(s_rest, c + 1)
                e.memset(feat[1][64:P, :, :], 0.0).then_inc(s_pad, 1)

            def chunk_pair(i, mode, at, less=0):
                if mode is PLAIN:
                    pad(2 * i + 1)
                for b in range(2):
                    g, k = at or (0, 0)
                    chunk(2 * i + b, b, 2 * i + b - less, mode, mode is not PLAIN or b == 0,
                          at and (g, (UNITS // 2 * g + k + 1) * 16 * len(SLOT_PARTS)), UNITS * g + 2 * k + b)

            def flush(g):
                e.wait_ge(s_sums, g + 1)
                e.wait_ge(s_share_out, 16 * (g + 1))
                for k in range(4):
                    n = min(2, GROUP_BLOCKS - 2 * k)
                    last = e.tensor_reduce(group_sum[:, 2 * k:2 * k + n, :],
                                           ps_share[k][:, 0:n * 3 * D].rearrange("p (a k d) -> p a d k", k=3, d=D),
                                           AX.X, ALU.add)
                last.then_inc(s_flush, 1)

            def prologue(c):
                split_rest(c, 0)
                split_lo(c, 0)

            prologue(0)
            to_slots(0, 0, range(SHARE))
            main_loop(e, chunk_pair, after_group=flush)
            read_window(N_CHUNKS, 0)
            add_window(N_CHUNKS, 0, N_CHUNKS)
            again = e.value_load(flag_i[0:1, 0:1], min_val=0, max_val=1)
            with e.If(again > 0):
                e.tensor_scalar(rows_code[1][:, :], rows_i[1][:, :], CODE, None, ALU.add).then_inc(s_codes, 1)
                e.tensor_scalar(cols_code[1][:, :, :], cols_f[1][:, :, :], float(CODE), None, ALU.add).then_inc(s_codes, 1)
                e.wait_ge(s_codes, 2)
                prologue(2 * PAIRS)
                with e.Fori(PAIRS, 2 * PAIRS - 1) as i:
                    chunk_pair(i, BY_DST, None, N_CHUNKS)
                pad(4 * PAIRS - 1)
                for b in range(2):
                    chunk(4 * PAIRS - 2 + b, b, N_CHUNKS - 2 + b, BY_DST, b == 0, None, 0)
                prologue(4 * PAIRS)
                with e.Fori(2 * PAIRS, 2 * PAIRS + SHARE_PAIRS - 1) as i:
                    chunk_pair(i, SHARE_BY_SRC, None, 2 * N_CHUNKS)
                for b in range(2):
                    c = 2 * (2 * PAIRS + SHARE_PAIRS - 1) + b
                    chunk(c, b, c - 2 * N_CHUNKS, SHARE_BY_SRC, b == 0, None, 0)
                e.wait_ge(s_wadd, N_CHUNKS + 3)
                with e.Fori(0, N_TILES) as i:
                    e.wait_ge(s_inT, i + 1)
                    cols = aggT[0:D, bass.ds(i * P, P)]
                    e.tensor_tensor(cols, cols, bank[0][0:D, 0:P], ALU.add).then_inc(s_ina, 1)
                e.wait_ge(s_ina, N_TILES + 1)
            e.wait_ge(s_wadd, N_CHUNKS + 3)
            e.sem_inc(s_in_ready, 1)
            e.sem_inc(s_tail, 1)

            def sum_tables(j, g, b):
                n = tiles_in(g)
                e.tensor_copy(x_out[b][:, 0:n, 0:D], tile_cols(xs, g, n)).then_inc(s_xg, 1)
                e.wait_ge(s_load[b], 16 * ALL_TABLES * (j + 1))
                e.tensor_reduce(x_out[b][:, 0:n, D:2 * D],
                                tabs[b][:, :, 0:n * D].rearrange("p k (r d) -> p r d k", d=D),
                                AX.X, ALU.add).then_inc(s_sum, 1)

            def group(j, g, b):
                n = tiles_in(g)
                e.wait_ge(s_o, g + 3)
                e.tensor_tensor(y_sum[:, 0:n, :], tile_cols(xs, g, n),
                                bank[6 + b][:, 0:n * P].rearrange("p (t d) -> p t d", d=P)[:, :, 0:D],
                                ALU.add).then_inc(s_y, 1)
                e.wait_ge(s_y, g + 3)
                e.tensor_tensor(y[:, 0:n, :], y_sum[:, 0:n, :],
                                b2s[:, :].rearrange("p (a d) -> p a d", a=1).to_broadcast([P, n, D]),
                                ALU.add).then_inc(s_yb, 1)
                e.wait_ge(s_yb, g + 1)
                for t in range(n):
                    last = e.bn_stats(stats[:, t, :], y[:, t, :])
                last.then_inc(s_st, 1)
                e.wait_ge(s_st, g + 1)
                e.nop(nofuse=True)
                for t in range(n):
                    last = e.bn_aggr(mv[:, t, :], stats[:, t, :])
                last.then_inc(s_mv, 1)
                e.wait_ge(s_mv, g + 1)
                e.tensor_scalar(var_eps[:, 0:n], mv[:, 0:n, 1], EPS, None, ALU.add).then_inc(s_ag, 1)
                if not isinstance(g, int) or g + 3 <= GROUPS:
                    e.wait_ge(s_nt, g + 2)
                    sum_tables(j + 1 + b, g + 3, 1 - b)
                e.wait_ge(s_rs, g + 1)
                for t in range(n):
                    last = e.tensor_scalar(tile_cols(xs, g, n)[:, t, :], y[:, t, :], mv[:, t, 0:1], rstd[:, t:t + 1],
                                           ALU.subtract, ALU.mult)
                last.then_inc(s_ln, 1)

            e.wait_ge(s_x, 32)
            e.wait_ge(s_w, 16 * W_LOADS)
            sum_tables(0, 0, 0)
            sum_tables(0, 1, 1)
            e.wait_ge(s_nt, 1)
            sum_tables(1, 2, 0)
            all_groups(e, group)

        @block.tensor
        def _(e):
            for w, (n, a, z) in enumerate(TBATCH):
                if w == 0:
                    e.wait_ge(s_cst, 16)
                if a == 0:
                    e.wait_ge(s_f[n], 1)
                if w >= 4:
                    e.wait_ge(s_te, w - 3)
                for j in range(a, z):
                    last = e.transpose(bank[w % 4][:, (j - a) * N_CHUNKS:(j - a + 1) * N_CHUNKS],
                                       rows_f[n][:, j::COLS], ident[0:N_CHUNKS, 0:N_CHUNKS])
                last.then_inc(s_tp, 1)
            e.wait_ge(s_one, 6)
            e.wait_ge(s_pre, 7)
            e.matmul(bank[4][:, 0:N_CHUNKS], ones[0:N_CHUNKS, :], diag[:, :], start=True, stop=True)
            e.matmul(bank[5][:, 0:1], ones[0:N_CHUNKS, :], wide[:, :], start=True, stop=True).then_inc(s_b, 1)
            e.wait_ge(s_pre, PRE_RANKS)
            counts = before[:, :, SHARE, :]
            e.matmul(bank[6][:, 0:SHARE_CHUNKS * NODE_GROUPS], above_bf[:, :], counts, start=True, stop=True)
            e.matmul(bank[7][:, 0:SHARE_CHUNKS * NODE_GROUPS], ones_bf[:, :], counts, start=True, stop=True).then_inc(s_ranks, 1)
            e.wait_ge(s_te, 2 * BATCHES)
            e.wait_ge(s_pre, PRE_FLAG)

            def window_to_columns(c, b):
                e.wait_ge(s_wsum, c + 2)
                e.wait_ge(s_wadd, c + 2)
                e.nop(nofuse=True)
                e.transpose(ps_winT, win_sum[1 - b][:, :], ident).then_inc(s_wT, 1)

            def spread(d, q, n):
                row = ident_bf[0:N_CHUNKS, bass.ds(d, 1)].to_broadcast([N_CHUNKS, P])
                v = rows_code[n][:, :].bitcast(bf16).rearrange("c (p q j) -> c q j p", q=QUADS, j=QUAD)
                e.matmul(ps_nodes[:, :], row, v[:, q, :, :], start=True, stop=True).then_inc(s_nodes, 1)

            def slot_round(c, b, r):
                e.wait_ge(s_slot_ev, ROUNDS * c + r + 1)
                if r == 0:
                    e.wait_ge(s_to_slot, c + 1)
                    e.wait_ge(s_nodes_in, c + 1)
                for g in range(2 * r, min(2 * r + 2, NODE_GROUPS)):
                    o = g % 2 * SLOT_W
                    for k in range(SHARE):
                        last = e.matmul(ps_share[r % 2][:, o:o + SLOT_W], to_slot[b][:, k, g * P:(g + 1) * P],
                                        parts[b][:, SHARE_FROM + k, 1:], start=(k == 0), stop=(k == SHARE - 1))
                last.then_inc(s_slot, 1)

            def sum_tile(u, b, i):
                e.wait_ge(s_to_node, UNIT_TILES * u + i + 1)
                for a in range(GROUP_BLOCKS):
                    last = e.matmul(ps_share[a // 2][:, a % 2 * 3 * D:(a % 2 + 1) * 3 * D],
                                    to_node[i % OH_BUFS][:, a * P:(a + 1) * P], slots_in[b][:, i, 0:3 * D],
                                    start=False, stop=False)
                last.then_inc(s_tile, 1)

            def zero_sums(g):
                e.wait_ge(s_flush, g + 1)
                e.wait_ge(s_slot_ev, ROUNDS * SHARE_CHUNKS + 2)
                for k in range(4):
                    e.matmul(ps_share[k][:, 0:6 * D], nothing[:, 0:P], nothing[:, :], start=True, stop=False)

            def end_sums(g):
                for k in range(4):
                    last = e.matmul(ps_share[k][:, 0:6 * D], nothing[:, 0:P], nothing[:, :], start=False, stop=True)
                last.then_inc(s_sums, 1)

            def chunk(c, b, d, mode, u, more):
                if not mode.window:
                    spread(d, 0, mode.n)
                e.wait_ge(s_lo, c + 1)
                for q in range(QUADS):
                    if q < len(mode.quads):
                        t0, n = mode.quads[q]
                        e.wait_ge(s_same, quad_no(c, mode) + q + 1)
                        if q + 1 < len(mode.quads):
                            spread(d, q + 1, mode.n)
                        e.wait_ge(s_ev, quad_no(c, mode) + q + 2)
                        for j in range(n):
                            t = t0 + j
                            o = j * (D + 1)
                            w = same[quad_buf(q, b, mode)][:, j, :]
                            e.matmul(ps_pay[:, o:o + D + 1], w, parts[b][:, t, 0:1 + D], start=True, stop=False)
                            for k in (1, 2):
                                last = e.matmul(ps_pay[:, o + 1:o + D + 1], w,
                                                parts[b][:, t, 1 + k * D:1 + (k + 1) * D], start=False, stop=(k == 2))
                        last.then_inc(s_pay, 1)
                    if mode.window and q == 0:
                        window_to_columns(c, b)
                    if more and mode.window and q == QUADS - 1:
                        spread(d + 1, 0, mode.n)
                    if mode.share:
                        slot_round(c, b, q)
                    if mode.window:
                        e.wait_ge(s_hot, QUADS * c + q + 1)
                        for j in range(QUAD):
                            t = QUAD * q + j
                            last = e.matmul(ps_win[:, 0:3 * D], onehot[q % 2][:, j, :], parts[b][:, t, 1:1 + 3 * D],
                                            start=(t == 0), stop=(t == COLS - 1))
                        last.then_inc(s_quad, 1)
                        if mode.sums:
                            for i in unit_tiles(q):
                                sum_tile(u, b, i)
                    else:
                        e.drain().then_inc(s_quad, 1)

            def chunk_pair(i, mode, at, less=0):
                g, k = at or (0, 0)
                for b in range(2):
                    chunk(2 * i + b, b, 2 * i + b - less, mode, UNITS * g + 2 * k + b, mode is not PLAIN or b == 0)

            e.matmul(ps_win[:, 0:3 * D], nothing[:, 0:P], nothing[:, 0:3 * D], start=True, stop=True)
            spread(0, 0, 0)
            main_loop(e, chunk_pair, before_group=zero_sums, after_group=end_sums)
            window_to_columns(N_CHUNKS, 0)
            again = e.value_load(flag_i[0:1, 0:1], min_val=0, max_val=1)
            with e.If(again > 0):
                e.wait_ge(s_codes, 2)
                with e.Fori(PAIRS, 2 * PAIRS) as i:
                    chunk_pair(i, BY_DST, None, N_CHUNKS)
                with e.Fori(2 * PAIRS, 2 * PAIRS + SHARE_PAIRS) as i:
                    chunk_pair(i, SHARE_BY_SRC, None, 2 * N_CHUNKS)
                with e.Fori(0, N_TILES) as i:
                    e.wait_ge(s_inl, 16 * i + 16)
                    e.wait_ge(s_ina, i + 1)
                    e.nop(nofuse=True)
                    e.transpose(bank[0][0:D, 0:P], in_now[:, :], ident).then_inc(s_inT, 1)
            e.sem_inc(s_tail, 1)

            def transposes(g, b):
                e.wait_ge(s_sum, g + 1)
                e.wait_ge(s_xg, g + 1)
                n = tiles_in(g)
                for t in range(n):
                    last = e.transpose(bank[b][:, t:n * P:n], x_out[b][:, t, :], ident)
                last.then_inc(s_nt, 1)

            def hidden(g, b):
                n = tiles_in(g)
                e.wait_ge(s_cat, g + 1)
                for m in range(2):
                    if not isinstance(g, int) or g > 0:
                        e.wait_ge(s_relu, 2 * g + m - 1)
                    h = bank[4 + m][:, 0:n * P]
                    e.matmul(h, w1io[:, m * P:(m + 1) * P], aggT[:, bass.ds(g * (GT * P), n * P)],
                             start=True, stop=False)
                    e.matmul(h, w1x[:, m * P:(m + 1) * P], xT[b][:, 0:n * P], start=False, stop=True).then_inc(s_h, 1)

            def group(j, g, b):
                n = tiles_in(g)
                if not isinstance(g, int) or g < GROUPS:
                    hidden(g + 1, 1 - b)
                if not isinstance(g, int) or g + 2 <= GROUPS:
                    transposes(g + 2, b)
                e.wait_ge(s_relu, 2 * g + 2)
                e.wait_ge(s_y, g + 1)
                for t in range(n):
                    for m in range(2):
                        last = e.matmul(bank[6 + b][:, t * P:(t + 1) * P], hid[b][:, m, t:n * P:n], w2s[:, m, :],
                                        start=(m == 0), stop=(m == 1))
                last.then_inc(s_o, 1)

            e.wait_ge(s_x, 32)
            e.wait_ge(s_w, 16 * W_LOADS)
            e.wait_ge(s_in_ready, 1)
            transposes(0, 0)
            hidden(0, 0)
            transposes(1, 1)
            all_groups(e, group)


def kernel(x, src, dst, edge_attr_64, L0_gnn_W1, L0_gnn_b1, L0_gnn_W2, L0_gnn_b2):
    import numpy as np
    from concourse import bacc
    from concourse.bass_utils import run_bass_kernel_spmd

    part = np.arange(P, dtype=np.float32)[:, None]
    consts = np.concatenate([np.eye(P, dtype=np.float32), np.tile(part.T, (P, 1)),
                             np.exp2(POW - part), np.exp2(part - POW), part, (part < part.T),
                             np.tile(np.arange(GROUP_NODES), (P, 1)),
                             np.tile(np.arange(NODE_GROUPS + 1) * GROUP_NODES, (P, 1)),
                             np.tile(np.arange(NODE_GROUPS) * P, (P, 1))], axis=1).astype(np.float32)
    inputs = {"x": x, "src": src, "dst": dst, "edge_attr": edge_attr_64, "w1": L0_gnn_W1, "b1": L0_gnn_b1,
              "w2": L0_gnn_W2, "b2": L0_gnn_b2, "consts": consts}
    arrays = {f"in_{k}": np.ascontiguousarray(v) for k, v in inputs.items()}
    nc = bacc.Bacc("TRN2", target_bir_lowering=False, num_devices=1)
    args = [nc.dram_tensor(k, v.shape, mybir.dt.from_np(v.dtype), kind="ExternalInput").ap()
            for k, v in arrays.items()]
    out = nc.dram_tensor("out", (N_NODES, D), mybir.dt.float32, kind="ExternalOutput").ap()
    build(nc, *args, out)
    r = run_bass_kernel_spmd(nc, [arrays], core_ids=[0])
    return r.results[0]["out"]
```
